# Optimizing a Trainium2 kernel written in Bass

```python
import numpy as np
import jax
import jax.numpy as jnp

def _softmax(x, axis=-1):
    return jax.nn.softmax(x, axis=axis)

def _gelu(x):
    return jax.nn.gelu(x, approximate=True)

def _silu(x):
    return jax.nn.silu(x)

def _sigmoid(x):
    return jax.nn.sigmoid(x)

def _layernorm(x, axis=-1, eps=1e-05):
    m = jnp.mean(x, axis=axis, keepdims=True)
    v = jnp.var(x, axis=axis, keepdims=True)
    return (x - m) / jnp.sqrt(v + eps)

def _scatter_add(tgt, idx, src, axis=0):
    return tgt.at[idx].add(src)

def _segment_sum(src, seg, n):
    return jax.ops.segment_sum(src, seg, n)
kernel_name = 'mk_prb_d1_jaxref_r4_e54384'

def setup_inputs(seed: int=0):
    np.random.seed(seed)
    _w = jnp.asarray

    def _L0_attn_setup():
        import jax, jax.numpy as jnp
        import numpy as np
        NUM_HEADS = 16
        ROPE_BASE = 10000.0

        def _rotate_half(x):
            xr = x.reshape(*x.shape[:-1], -1, 2)
            x1, x2 = (xr[..., 0], xr[..., 1])
            return jnp.stack((-x2, x1), axis=-1).reshape(x.shape)

        def _rope(x):
            hd = x.shape[-1]
            n = x.shape[-2]
            inv_freq = 1.0 / ROPE_BASE ** (jnp.arange(0, hd, 2, dtype=jnp.float32) / hd)
            freqs = jnp.outer(jnp.arange(n, dtype=jnp.float32), inv_freq)
            freqs = jnp.repeat(freqs, 2, axis=-1)
            return x * jnp.cos(freqs) + _rotate_half(x) * jnp.sin(freqs)
        key = jax.random.key(seed)
        k0, k1, k2 = jax.random.split(key, 3)
        B, N, D = (2, 512, 256)
        X = jax.random.normal(k0, (B, N, D), jnp.float32)
        Wqkv = jax.random.normal(k1, (D, 3 * D), jnp.float32) * D ** (-0.5)
        Wout = jax.random.normal(k2, (D, D), jnp.float32) * D ** (-0.5)
        bout = jnp.zeros((D,), jnp.float32)
        return {'X': X, 'Wqkv': Wqkv, 'Wout': Wout, 'bout': bout}
    _L0_attn_in = _L0_attn_setup()

    def _L0_ffn_setup():
        import jax, jax.numpy as jnp
        import numpy as np
        NUM_TRUE = 8
        NUM_NULL = 2
        NUM_EXPERTS = NUM_TRUE + NUM_NULL
        TOP_K = 2
        key = jax.random.key(seed)
        k0, k1, k2 = jax.random.split(key, 3)
        B, S, D = (4, 512, 256)
        inputs = jax.random.normal(k0, (B, S, D), dtype=jnp.float32)
        gate_w = jax.random.normal(k1, (NUM_EXPERTS, D), dtype=jnp.float32) * 0.02
        gate_b = jnp.zeros((NUM_EXPERTS,), dtype=jnp.float32)
        expert_w = jax.random.normal(k2, (NUM_TRUE, D, D), dtype=jnp.float32) * 0.02
        expert_b = jnp.zeros((NUM_TRUE, D), dtype=jnp.float32)
        return {'inputs': inputs, 'gate_w': gate_w, 'gate_b': gate_b, 'expert_w': expert_w, 'expert_b': expert_b}
    _L0_ffn_in = _L0_ffn_setup()
    _d = {'L0_attn_X': _L0_attn_in['X'], 'L0_attn_Wqkv': _L0_attn_in['Wqkv'], 'L0_attn_Wout': _L0_attn_in['Wout'], 'L0_attn_bout': _L0_attn_in['bout'], 'L0_ffn_gate_w': _L0_ffn_in['gate_w'], 'L0_ffn_gate_b': _L0_ffn_in['gate_b'], 'L0_ffn_expert_w': _L0_ffn_in['expert_w'], 'L0_ffn_expert_b': _L0_ffn_in['expert_b']}
    _x0 = _d['L0_attn_X']
    _d['L0_attn_X'] = jax.random.normal(jax.random.fold_in(jax.random.key(seed), 1), (2, 2048, 256), dtype=_x0.dtype)
    del _x0
    return _d

def reference(L0_attn_X, L0_attn_Wqkv, L0_attn_Wout, L0_attn_bout, L0_ffn_gate_w, L0_ffn_gate_b, L0_ffn_expert_w, L0_ffn_expert_b):

    def _L0_attn_ref(X, Wqkv, Wout, bout):
        import jax, jax.numpy as jnp
        import numpy as np
        NUM_HEADS = 16
        ROPE_BASE = 10000.0

        def _rotate_half(x):
            xr = x.reshape(*x.shape[:-1], -1, 2)
            x1, x2 = (xr[..., 0], xr[..., 1])
            return jnp.stack((-x2, x1), axis=-1).reshape(x.shape)

        def _rope(x):
            hd = x.shape[-1]
            n = x.shape[-2]
            inv_freq = 1.0 / ROPE_BASE ** (jnp.arange(0, hd, 2, dtype=jnp.float32) / hd)
            freqs = jnp.outer(jnp.arange(n, dtype=jnp.float32), inv_freq)
            freqs = jnp.repeat(freqs, 2, axis=-1)
            return x * jnp.cos(freqs) + _rotate_half(x) * jnp.sin(freqs)
        B, N, D = X.shape
        H = NUM_HEADS
        hd = D // H
        scale = hd ** (-0.5)
        qkv = X @ Wqkv
        q, k, v = jnp.split(qkv, 3, axis=-1)

        def to_heads(t):
            return t.reshape(B, N, H, hd).transpose(0, 2, 1, 3)
        Q, K, V = (to_heads(q), to_heads(k), to_heads(v))
        Q = _rope(Q)
        K = _rope(K)
        scores = jnp.einsum('bhnd,bhmd->bhnm', Q, K) * scale
        causal = jnp.tril(jnp.ones((N, N), dtype=bool))
        scores = jnp.where(causal, scores, -jnp.inf)
        attn = jax.nn.softmax(scores, axis=-1)
        out = jnp.einsum('bhnm,bhmd->bhnd', attn, V)
        out = out.transpose(0, 2, 1, 3).reshape(B, N, D)
        return out @ Wout + bout

    def _L0_ffn_ref(inputs, gate_w, gate_b, expert_w, expert_b):
        import jax, jax.numpy as jnp
        import numpy as np
        NUM_TRUE = 8
        NUM_NULL = 2
        NUM_EXPERTS = NUM_TRUE + NUM_NULL
        TOP_K = 2
        D = inputs.shape[-1]
        x = inputs.reshape(-1, D)
        gate_logits = x @ gate_w.T + gate_b
        gate_probs = jax.nn.softmax(gate_logits, axis=-1)
        weights, selected = jax.lax.top_k(gate_probs, TOP_K)
        true_mask = selected < NUM_TRUE
        true_weights = weights * true_mask
        denom = true_weights.sum(axis=-1, keepdims=True)
        denom = jnp.where(denom > 0, denom, jnp.ones_like(denom))
        norm_w = (true_weights / denom).astype(x.dtype)
        one_hot = jax.nn.one_hot(selected, NUM_EXPERTS, dtype=norm_w.dtype)
        combine_w = jnp.einsum('tk,tke->te', norm_w, one_hot)[:, :NUM_TRUE]
        expert_out = jnp.einsum('td,edh->teh', x, expert_w) + expert_b[None, :, :]
        out = jnp.einsum('te,teh->th', combine_w, expert_out)
        return out.reshape(inputs.shape[:-1] + (out.shape[-1],))
    x = L0_attn_X
    xn = _layernorm(x, axis=-1)
    x = x + _L0_attn_ref(xn, L0_attn_Wqkv, L0_attn_Wout, L0_attn_bout) + _L0_ffn_ref(xn, L0_ffn_gate_w, L0_ffn_gate_b, L0_ffn_expert_w, L0_ffn_expert_b)
    return x

_drawn_inputs = setup_inputs


def setup_inputs(seed=0):
    import zlib

    import numpy as np

    out = dict(_drawn_inputs(seed))
    spreads = {'L0_attn_bout': (0.0, 0.1), 'L0_ffn_gate_b': (0.0, 0.1), 'L0_ffn_expert_b': (0.0, 0.1)}
    factors = {}
    for name, (base, spread) in spreads.items():
        noise = np.random.default_rng([zlib.crc32(name.encode()), seed]).standard_normal(out[name].shape)
        drawn = base * np.exp(spread * noise) if base else spread * noise
        out[name] = jnp.asarray(drawn.astype(out[name].dtype))
    for name, factor in factors.items():
        out[name] = (out[name] * factor).astype(out[name].dtype)
    return out
```

```python
from contextlib import ExitStack

import numpy as np

import concourse.bass as bass
from concourse import mybir

ALU = mybir.AluOpType
ACT = mybir.ActivationFunctionType
AX = mybir.AxisListType
F32 = mybir.dt.float32
BF16 = mybir.dt.bfloat16
U32 = mybir.dt.uint32

P = 128
B, N, D = 2, 2048, 256
HEADS, HD = 16, 16
EXPERTS, GATES = 8, 10
EPS = 1e-5
SCALE = HD ** -0.5
KC = D // P
TT = N // P
TILES = B * TT
CH = 512
CT = CH // P
CHUNKS = N // CH
QKT = 2 * D // P
HG = 4
GROUPS = B * HEADS // HG
GR = HG * HD
VW = 32
Q_PART = (0, 0, 0, 1, 1, 2)
K_PART = (0, 1, 2, 0, 1, 0)
PR = len(Q_PART) * HD
MR = 3
LOW = -3.0e38
ONE = 1


def project(nc, x, wqk, wvg, we, be, bout, gb, cos, sin, qk_s, v_s, acc):
    with ExitStack() as ctx:
        sb = lambda n, s, d=F32: ctx.enter_context(nc.sbuf_tensor(n, s, d))
        sems = []

        def sem(n):
            sems.append(ctx.enter_context(nc.semaphore(n)))
            return sems[-1]

        pair = lambda n: [sem(f"{n}{i}") for i in range(2)]

        ident = sb("ident", [P, P])
        wqk_sb = sb("wqk_sb", [P, KC, 2 * D])
        wvg_sb = sb("wvg_sb", [P, KC, D + GATES])
        we_sb = sb("we_sb", [P, KC, EXPERTS * D])
        be_sb = sb("be_sb", [EXPERTS + 1, D])
        gb_sb = sb("gb_sb", [P, GATES])
        trig = sb("trig", [P, 2, CH])
        iota = sb("iota", [P, GATES])
        eps = sb("eps", [P, 1])
        xs = [sb(f"xs{i}", [P, CT, D]) for i in range(2)]
        xn = [sb(f"xn{i}", [P, CT, D]) for i in range(2)]
        xnT = [sb(f"xnT{i}", [P, KC, CH]) for i in range(2)]
        stat = sb("stat", [P, CT, 6])
        mv = sb("mv", [P, CT, 2])
        std = sb("std", [P, CT])
        rstd = sb("rstd", [P, CT])
        vst = [sb(f"vst{i}", [P, CT, HEADS, VW]) for i in range(2)]
        lg = [sb(f"lg{i}", [P, CT, GATES]) for i in range(2)]
        gl = sb("gl", [P, CT, GATES])
        ge = sb("ge", [P, CT, GATES])
        gp = sb("gp", [P, CT, GATES])
        gm = sb("gm", [P, CT])
        gr = sb("gr", [P, CT])
        top = sb("top", [P, CT, 8])
        topi = sb("topi", [P, CT, 8], U32)
        topf = sb("topf", [P, CT, 2])
        hot = sb("hot", [P, 2, CT, GATES])
        cw = sb("cw", [P, CT, EXPERTS])
        den = sb("den", [P, CT])
        dez = sb("dez", [P, CT])
        c9 = [sb(f"c9{i}", [P, CT, EXPERTS + 1]) for i in range(2)]
        c9T = sb("c9T", [EXPERTS + 1, CH])
        odd = [sb(f"odd{i}", [P, D]) for i in range(2)]
        rot = [sb(f"rot{i}", [P, CH]) for i in range(2)]
        swp = [sb(f"swp{i}", [P, CH]) for i in range(2)]
        part = [sb(f"part{i}", [P, 3, CH], BF16) for i in range(2)]

        psT = ctx.enter_context(nc.psum_tensor("psT", [P, 2, CH], F32))
        psQ = ctx.enter_context(nc.psum_tensor("psQ", [P, 2, CH], F32))
        psM = ctx.enter_context(nc.psum_tensor("psM", [P, 2, CH], F32))
        psC = ctx.enter_context(nc.psum_tensor("psC", [P, CH], F32))
        psB = ctx.enter_context(nc.psum_tensor("psB", [P, D], F32))

        x_in = pair("x_in")
        acc_stored = pair("acc_stored")
        w_in = sem("w_in")
        w2_in = sem("w2_in")
        trig_in = sem("trig_in")
        const = sem("const")
        vcol = sem("vcol")
        stats = sem("stats")
        std_ok = sem("std_ok")
        xn_ok = sem("xn_ok")
        xT_ps = sem("xT_ps")
        xT_ok = sem("xT_ok")
        vg_ps = sem("vg_ps")
        vg_ok = sem("vg_ok")
        v_stored = pair("v_stored")
        gate_in = sem("gate_in")
        gate_e = sem("gate_e")
        gate_c = sem("gate_c")
        qk_ps = sem("qk_ps")
        rope_ok = pair("rope_ok")
        split_ok = pair("split_ok")
        part_stored = pair("part_stored")
        moe_ps = sem("moe_ps")
        moe_read = pair("moe_read")
        cT_ps = sem("cT_ps")
        cT_ok = sem("cT_ok")
        bias_ps = sem("bias_ps")
        bias_read = sem("bias_read")
        acc_ok = sem("acc_ok")
        carrier = sem("carrier")
        dve_step = sem("dve_step")
        pool_step = sem("pool_step")

        NB = B
        block = ctx.enter_context(nc.Block())

        @block.sync
        def _(sp):
            def load_x(j, b):
                sp.dma_start(xs[b][:, :, :],
                             x[b, bass.ds(j * CH, CH), :].rearrange("(t p) d -> p t d", p=P)).then_inc(x_in[b], 16)

            def load_trig(j):
                sp.dma_start(trig[:, 0, :], cos[:, bass.ds(j * CH, CH)]).then_inc(trig_in, 16)
                sp.dma_start(trig[:, 1, :], sin[:, bass.ds(j * CH, CH)]).then_inc(trig_in, 16)

            load_x(0, 0)
            sp.dma_start(wvg_sb[:, :, :], wvg.rearrange("(k p) n -> p k n", p=P)).then_inc(w_in, 16)
            sp.dma_start(wqk_sb[:, :, :], wqk.rearrange("(k p) n -> p k n", p=P)).then_inc(w_in, 16)
            sp.dma_start(gb_sb[:, :], gb.partition_broadcast(P)).then_inc(w_in, 16)
            load_trig(0)
            load_x(0, 1)
            for e in range(EXPERTS):
                sp.dma_start(we_sb[:, :, e * D:(e + 1) * D],
                             we[e].rearrange("(k p) n -> p k n", p=P)).then_inc(w2_in, 16)
            sp.dma_start(be_sb[0:EXPERTS, :], be).then_inc(w2_in, 16)
            sp.dma_start(be_sb[EXPERTS:EXPERTS + 1, :], bout).then_inc(w2_in, 16)

            def body(j, last):
                for b in range(NB):
                    for k in range(QKT):
                        sp.wait_ge(split_ok[k % 2], ONE + (2 * j + b) * 2 + k // 2 + 1)
                        sp.dma_start(qk_s[k // 2, :, bass.ds(b * D + k % 2 * P, P), bass.ds(j * CH, CH)]
                                     .rearrange("s p n -> p s n"), part[k % 2][:, :, :]).then_inc(part_stored[k % 2], 16)
                    sp.wait_ge(vg_ok, ONE + (2 * j + b) * CT + CT)
                    for h in range(HEADS // HG):
                        sp.dma_start(v_s[b * (HEADS // HG) + h, :, bass.ds(j * CT, CT), :],
                                     vst[b][:, :, h * HG:(h + 1) * HG, :].rearrange("p t h w -> p t (h w)")
                                     ).then_inc(v_stored[b], 16)
                    if b == 1 and not last:
                        for i in range(2):
                            sp.wait_ge(rope_ok[i], ONE + 4 * j + 4)
                            sp.wait_ge(split_ok[i], ONE + 4 * j + 4)
                        sp.sem_inc(carrier, 1)
                        load_trig(j + 1)
                    sp.wait_ge(acc_ok, ONE + (2 * j + b) * CT + CT)
                    sp.dma_start(acc[:, bass.ds(j * CT + b * TT, CT), :], xs[b][:, :, :]).then_inc(acc_stored[b], 16)
                    if not last:
                        sp.wait_ge(acc_stored[b], ONE + 16 * j + 16)
                        load_x(j + 1, b)

            with sp.Fori(0, CHUNKS - 1) as j:
                body(j, False)
            body(CHUNKS - 1, True)
            for b in range(2):
                sp.wait_ge(acc_stored[b], ONE + 16 * CHUNKS)
                sp.wait_ge(v_stored[b], ONE + 16 * (HEADS // HG) * CHUNKS)
                sp.wait_ge(part_stored[b], ONE + 16 * 4 * CHUNKS)

        @block.gpsimd
        def _(pool):
            for every in sems:
                pool.sem_inc(every, ONE)
            steps = [0]

            def step(ins):
                steps[0] += 1
                return ins.then_inc(pool_step, 1)

            step(nc.gpsimd.memset(ident[:, :], 0.0))
            pool.wait_ge(pool_step, ONE + 1)
            nc.gpsimd.affine_select(out=ident[:, :], in_=ident[:, :], compare_op=ALU.not_equal, fill=1.0, base=0,
                                    pattern=[[-1, P]], channel_multiplier=1).then_inc(const, 1)
            nc.gpsimd.iota(iota[:, :], pattern=[[1, GATES]], base=0, channel_multiplier=0,
                           allow_small_or_imprecise_dtypes=True).then_inc(const, 1)
            nc.gpsimd.memset(eps[:, :], EPS).then_inc(const, 1)
            for b in range(NB):
                nc.gpsimd.memset(vst[b][:, :, :, :], 1.0).then_inc(const, 1)
                nc.gpsimd.memset(c9[b][:, :, :], 1.0).then_inc(const, 1)
            STEPS = 5

            def body(j):
                pool.wait_ge(trig_in, ONE + 32 * j + 32)
                for b in range(NB):
                    for k in range(QKT):
                        i, use = k % 2, (2 * j + b) * 2 + k // 2
                        at = 1 + ((2 * j + b) * QKT + k) * STEPS
                        a, s, o = rot[i][:, :], swp[i][:, :], part[i]
                        pool.wait_ge(rope_ok[i], ONE + use + 1)
                        step(nc.gpsimd.tensor_tensor(s, s, trig[:, 1, :], ALU.mult))
                        pool.wait_ge(pool_step, ONE + at + 1)
                        step(nc.gpsimd.tensor_tensor(a, a, s, ALU.add))
                        pool.wait_ge(part_stored[i], ONE + 16 * use)
                        pool.wait_ge(pool_step, ONE + at + 2)
                        pool.sem_inc(carrier, 1)
                        step(nc.gpsimd.tensor_copy(o[:, 0, :], a))
                        pool.wait_ge(pool_step, ONE + at + 3)
                        step(nc.gpsimd.tensor_tensor(a, a, o[:, 0, :], ALU.subtract))
                        pool.wait_ge(pool_step, ONE + at + 4)
                        pool.sem_inc(carrier, 1)
                        step(nc.gpsimd.tensor_copy(o[:, 1, :], a))
                        pool.wait_ge(pool_step, ONE + at + 5)
                        nc.gpsimd.tensor_tensor(o[:, 2, :], a, o[:, 1, :], ALU.subtract).then_inc(split_ok[i], 1)

            with pool.Fori(0, CHUNKS) as j:
                body(j)

        @block.scalar
        def _(act):
            def deviation(s):
                act.wait_ge(stats, ONE + s + 1)
                nc.scalar.activation(std[:, :], mv[:, :, 1], ACT.Sqrt, bias=eps[:, :]).then_inc(std_ok, 1)

            def copy_xT(s, b):
                for k in range(KC):
                    act.wait_ge(xT_ps, ONE + KC * s + k + 1)
                    nc.scalar.copy(xnT[b][:, k, :], psT[:, k, :]).then_inc(xT_ok, 1)

            act.wait_ge(const, ONE + 7)
            deviation(0)
            copy_xT(0, 0)

            def body(j, last):
                for b in range(NB):
                    s = 2 * j + b
                    act.wait_ge(v_stored[b], ONE + 16 * (HEADS // HG) * j)
                    for t in range(CT):
                        act.wait_ge(vg_ps, ONE + CT * s + t + 1)
                        nc.scalar.copy(vst[b][:, t, :, 0:HD],
                                       psT[:, t % 2, 0:D].rearrange("p (h d) -> p h d", d=HD)).then_inc(vcol, 1)
                        nc.scalar.copy(lg[b][:, t, :], psT[:, t % 2, D:D + GATES]).then_inc(vg_ok, 1)
                    act.wait_ge(gate_in, ONE + s + 1)
                    nc.scalar.activation(ge[:, :, :], gl[:, :, :], ACT.Exp).then_inc(gate_e, 1)
                    if not (last and b == 1):
                        deviation(s + 1)
                        copy_xT(s + 1, 1 - b)

            with act.Fori(0, CHUNKS - 1) as j:
                body(j, False)
            body(CHUNKS - 1, True)

        @block.vector
        def _(dve):
            n = [0]

            def step(ins):
                n[0] += 1
                return ins.then_inc(dve_step, 1)

            def norm_a(j, b):
                dve.wait_ge(x_in[b], ONE + 16 * j + 16)
                for t in range(CT):
                    step(nc.vector.bn_stats(stat[:, t, :], xs[b][:, t, :]))

            def norm_b(base):
                for t in range(CT):
                    dve.wait_ge(dve_step, ONE + base + t + 1)
                    dve.sem_inc(carrier, 1)
                    ins = nc.vector.bn_aggr(mv[:, t, :], stat[:, t, :])
                ins.then_inc(stats, 1)

            def norm_c(s, b, base, before=None):
                dve.wait_ge(std_ok, ONE + s + 1)
                step(nc.vector.reciprocal(rstd[:, :], std[:, :]))
                dve.wait_ge(dve_step, ONE + base + 1)
                if before is not None:
                    dve.wait_ge(xT_ps, ONE + KC * before)
                for t in range(CT):
                    ins = nc.vector.tensor_scalar(xn[b][:, t, :], xs[b][:, t, :], mv[:, t, 0:1], rstd[:, t:t + 1],
                                                  ALU.subtract, ALU.mult)
                ins.then_inc(xn_ok, 1)

            SWAP = [i ^ 1 for i in range(32)]

            def rope(s, k):
                i, use = k % 2, 2 * s + k // 2
                dve.wait_ge(qk_ps, ONE + QKT * s + k + 1)
                dve.wait_ge(split_ok[i], ONE + use)
                dve.sem_inc(carrier, 1)
                nc.vector.stream_shuffle(swp[i][:, :], psQ[:, i, :], SWAP)
                nc.vector.tensor_tensor(rot[i][:, :], psQ[:, i, :], trig[:, 0, :], ALU.mult).then_inc(rope_ok[i], 1)

            def wide(a):
                return a.unsqueeze(2).to_broadcast([P, CT, GATES])

            def gates_a(s, b, base):
                dve.wait_ge(vg_ok, ONE + CT * s + CT)
                step(nc.vector.tensor_tensor(gl[:, :, :], lg[b][:, :, :],
                                             gb_sb[:, :].unsqueeze(1).to_broadcast([P, CT, GATES]), ALU.add))
                dve.wait_ge(dve_step, ONE + base + 1)
                step(nc.vector.tensor_reduce(gm[:, :], gl[:, :, :], AX.X, ALU.max))
                dve.wait_ge(dve_step, ONE + base + 2)
                nc.vector.tensor_tensor(gl[:, :, :], gl[:, :, :], wide(gm[:, :]), ALU.subtract).then_inc(gate_in, 1)

            def gates_b(s, b, base):
                dve.wait_ge(gate_e, ONE + s + 1)
                step(nc.vector.tensor_reduce(gr[:, :], ge[:, :, :], AX.X, ALU.add))
                dve.wait_ge(dve_step, ONE + base + 1)
                step(nc.vector.reciprocal(gr[:, :], gr[:, :]))
                dve.wait_ge(dve_step, ONE + base + 2)
                step(nc.vector.tensor_tensor(gp[:, :, :], ge[:, :, :], wide(gr[:, :]), ALU.mult))
                dve.wait_ge(dve_step, ONE + base + 3)
                for t in range(CT):
                    dve.sem_inc(carrier, 1)
                    step(nc.vector.max(top[:, t, :], gp[:, t, :]))
                for t in range(CT):
                    dve.wait_ge(dve_step, ONE + base + 4 + t)
                    dve.sem_inc(carrier, 1)
                    step(nc.vector.max_index(topi[:, t, :], top[:, t, :], gp[:, t, :]))
                dve.wait_ge(dve_step, ONE + base + 11)
                step(nc.vector.tensor_copy(topf[:, :, :], topi[:, :, 0:2]))
                dve.wait_ge(dve_step, ONE + base + 12)
                for i in range(2):
                    step(nc.vector.tensor_tensor(hot[:, i, :, :], iota[:, :].unsqueeze(1).to_broadcast([P, CT, GATES]),
                                                 topf[:, :, i:i + 1].to_broadcast([P, CT, GATES]), ALU.is_equal))
                dve.wait_ge(dve_step, ONE + base + 14)
                step(nc.vector.tensor_tensor(hot[:, 0, :, :], hot[:, 0, :, :], hot[:, 1, :, :], ALU.add))
                dve.wait_ge(dve_step, ONE + base + 15)
                step(nc.vector.tensor_tensor(cw[:, :, :], gp[:, :, 0:EXPERTS], hot[:, 0, :, 0:EXPERTS], ALU.mult))
                dve.wait_ge(dve_step, ONE + base + 16)
                step(nc.vector.tensor_reduce(den[:, :], cw[:, :, :], AX.X, ALU.add))
                dve.wait_ge(dve_step, ONE + base + 17)
                step(nc.vector.tensor_single_scalar(dez[:, :], den[:, :], 0.0, ALU.is_le))
                dve.wait_ge(dve_step, ONE + base + 18)
                step(nc.vector.tensor_tensor(den[:, :], den[:, :], dez[:, :], ALU.add))
                dve.wait_ge(dve_step, ONE + base + 19)
                step(nc.vector.reciprocal(den[:, :], den[:, :]))
                dve.wait_ge(dve_step, ONE + base + 20)
                nc.vector.tensor_tensor(c9[b][:, :, 0:EXPERTS], cw[:, :, :],
                                        den[:, :].unsqueeze(2).to_broadcast([P, CT, EXPERTS]), ALU.mult
                                        ).then_inc(gate_c, 1)

            def combine(s, b, t, base):
                dve.wait_ge(gate_c, ONE + s + 1)
                for n4 in range(EXPERTS // 2):
                    slot, uses = n4 % 2, (EXPERTS // 4) * (CT * s + t)
                    dve.wait_ge(moe_ps, ONE + (EXPERTS // 2) * (CT * s + t) + n4 + 1)
                    e = 2 * n4
                    if n4 > 0:
                        dve.wait_ge(dve_step, ONE + base + n4)
                    step(nc.vector.scalar_tensor_tensor(out=xs[b][:, t, :], in0=psM[:, slot, 0:D],
                                                        scalar=c9[b][:, t, e:e + 1], in1=xs[b][:, t, :],
                                                        op0=ALU.mult, op1=ALU.add))
                    if n4 == 0:
                        ins = nc.vector.tensor_scalar(odd[t % 2][:, :], psM[:, slot, D:2 * D],
                                                      c9[b][:, t, e + 1:e + 2], None, ALU.mult)
                    else:
                        dve.wait_ge(moe_read[1 - slot], ONE + uses + (n4 - 1) // 2 + 1)
                        ins = nc.vector.scalar_tensor_tensor(out=odd[t % 2][:, :], in0=psM[:, slot, D:2 * D],
                                                             scalar=c9[b][:, t, e + 1:e + 2], in1=odd[t % 2][:, :],
                                                             op0=ALU.mult, op1=ALU.add)
                    ins.then_inc(moe_read[slot], 1)
                dve.wait_ge(bias_ps, ONE + CT * s + t + 1)
                dve.wait_ge(moe_read[1], ONE + uses + EXPERTS // 4)
                nc.vector.tensor_tensor(odd[t % 2][:, :], psB[:, :], odd[t % 2][:, :], ALU.add
                                        ).then_inc(bias_read, 1)
                dve.wait_ge(dve_step, ONE + base + EXPERTS // 2)
                dve.wait_ge(bias_read, ONE + CT * s + t + 1)
                nc.vector.tensor_tensor(xs[b][:, t, :], xs[b][:, t, :], odd[t % 2][:, :], ALU.add).then_inc(acc_ok, 1)

            GA, GB, CB, NA, NCC = 2, 20, EXPERTS // 2, CT, 1
            FIRST = NA + NCC
            EACH = GA + GB + CT * CB + NA + NCC

            dve.wait_ge(const, ONE + 7)
            dve.wait_ge(w_in, ONE + 48)
            norm_a(0, 0)
            norm_b(0)
            norm_c(0, 0, NA)

            def body(j, last):
                dve.wait_ge(trig_in, ONE + 32 * j + 32)
                for b in range(NB):
                    s = 2 * j + b
                    at = FIRST + EACH * s
                    more = not (last and b == 1)
                    gates_a(s, b, at)
                    rope(s, 0)
                    rope(s, 1)
                    gates_b(s, b, at + GA)
                    rope(s, 2)
                    rope(s, 3)
                    dve.wait_ge(cT_ps, ONE + s + 1)
                    nc.vector.tensor_copy(c9T[:, :], psC[0:EXPERTS + 1, :]).then_inc(cT_ok, 1)
                    at = at + GA + GB
                    if more:
                        norm_a(j + b, 1 - b)
                        norm_b(at)
                        at = at + NA
                    combine(s, b, 0, at)
                    at = at + CB
                    if more:
                        norm_c(s + 1, 1 - b, at, before=s)
                        at = at + NCC
                    for t in range(1, CT):
                        combine(s, b, t, at)
                        at = at + CB

            with dve.Fori(0, CHUNKS - 1) as j:
                body(j, False)
            body(CHUNKS - 1, True)

        @block.tensor
        def _(pe):
            def transposes(s, b):
                pe.wait_ge(xn_ok, ONE + s + 1)
                for k in range(KC):
                    for t in range(CT):
                        ins = pe.transpose(psT[:, k, t * P:(t + 1) * P], xn[b][:, t, k * P:(k + 1) * P], ident[:, :])
                    ins.then_inc(xT_ps, 1)

            pe.wait_ge(const, ONE + 7)
            transposes(0, 0)
            pe.wait_ge(w_in, ONE + 48)

            def body(j, last):
                for b in range(NB):
                    s = 2 * j + b
                    pe.wait_ge(xT_ok, ONE + KC * s + KC)
                    for t in range(CT):
                        if t >= 2:
                            pe.wait_ge(vg_ok, ONE + CT * s + t - 1)
                        for k in range(KC):
                            ins = pe.matmul(psT[:, t % 2, 0:D + GATES], xnT[b][:, k, t * P:(t + 1) * P],
                                            wvg_sb[:, k, :], start=(k == 0), stop=(k == KC - 1))
                        ins.then_inc(vg_ps, 1)
                    for q in range(QKT):
                        pe.wait_ge(rope_ok[q % 2], ONE + 2 * s + q // 2)
                        for k in range(KC):
                            ins = pe.matmul(psQ[:, q % 2, :], wqk_sb[:, k, q * P:(q + 1) * P], xnT[b][:, k, :],
                                            start=(k == 0), stop=(k == KC - 1))
                        ins.then_inc(qk_ps, 1)
                    if b == 0:
                        pe.wait_ge(w2_in, ONE + 16 * (EXPERTS + 2))
                    for t in range(CT):
                        for n4 in range(EXPERTS // 2):
                            pe.wait_ge(moe_read[n4 % 2], ONE + (EXPERTS // 4) * (CT * s + t) + n4 // 2)
                            for k in range(KC):
                                ins = pe.matmul(psM[:, n4 % 2, :], xnT[b][:, k, t * P:(t + 1) * P],
                                                we_sb[:, k, n4 * 2 * D:(n4 + 1) * 2 * D],
                                                start=(k == 0), stop=(k == KC - 1))
                            ins.then_inc(moe_ps, 1)
                            if t == 0 and n4 == 1:
                                pe.wait_ge(gate_c, ONE + s + 1)
                                pe.wait_ge(cT_ok, ONE + s)
                                for u in range(CT):
                                    ins = pe.transpose(psC[0:EXPERTS + 1, u * P:(u + 1) * P], c9[b][:, u, :],
                                                       ident[:, :])
                                ins.then_inc(cT_ps, 1)
                        if t == 0:
                            pe.wait_ge(cT_ok, ONE + s + 1)
                        pe.wait_ge(bias_read, ONE + CT * s + t)
                        pe.matmul(psB[:, :], c9T[:, t * P:(t + 1) * P], be_sb[:, :], start=True, stop=True
                                  ).then_inc(bias_ps, 1)
                        if t == 1 and not (last and b == 1):
                            transposes(s + 1, 1 - b)

            with pe.Fori(0, CHUNKS - 1) as j:
                body(j, False)
            body(CHUNKS - 1, True)


def attend(nc, qk_s, v_s, aT):
    with ExitStack() as ctx:
        sb = lambda n, s, d=F32: ctx.enter_context(nc.sbuf_tensor(n, s, d))
        sems = []

        def sem(n):
            sems.append(ctx.enter_context(nc.semaphore(n)))
            return sems[-1]

        pair = lambda n: [sem(f"{n}{i}") for i in range(2)]

        Qs = [sb(f"Qs{i}", [PR + MR, HG, N], BF16) for i in range(2)]
        Ks = [sb(f"Ks{i}", [PR + MR, HG, N], BF16) for i in range(2)]
        Vs = [sb(f"Vs{i}", [P, TT, HG * VW]) for i in range(2)]
        probs = [sb(f"probs{i}", [P, HG, CH]) for i in range(2)]
        causal = sb("causal", [P, 2 * CH], BF16)
        trash = sb("trash", [P, 2, 2 * CH], BF16)
        blk = sb("blk", [P, HG * TT, 2])
        nm = sb("nm", [P, HG * TT])
        nmp = sb("nmp", [P, MR + 1, HG * TT], BF16)
        nmT = sb("nmT", [P, 2, P], BF16)
        identb = sb("identb", [P, P], BF16)
        ot = [sb(f"ot{i}", [P, CH]) for i in range(2)]
        rsum = [sb(f"rsum{i}", [P, CH]) for i in range(2)]
        on = [sb(f"on{i}", [P, CH]) for i in range(2)]

        SB = 3
        psS = ctx.enter_context(nc.psum_tensor("psS", [P, SB, CH], F32))
        psP = ctx.enter_context(nc.psum_tensor("psP", [P, 2, 2 * CH], F32))
        psO = ctx.enter_context(nc.psum_tensor("psO", [P, CH], F32))

        kv_in = [[sem(f"kv_in{i}{q}") for q in range(CHUNKS)] for i in range(2)]
        m_in = pair("m_in")
        const = sem("const_b")
        s_ps = sem("s_ps")
        s_read = [sem(f"s_read{i}") for i in range(SB)]
        masked = sem("masked")
        pv_ok = pair("pv_ok")
        o_copied = sem("o_copied")
        o_norm = pair("o_norm")
        rs_ok = pair("rs_ok")
        o_stored = pair("o_stored")
        quarter = sem("quarter")
        first_ps = pair("first_ps")
        first_ok = pair("first_ok")
        mt_ps = sem("mt_ps")
        mt_ok = sem("mt_ok")
        carrier = sem("carrier_b")
        m_step = sem("m_step")
        r_step = sem("r_step")
        pool_b = sem("pool_b")

        units = [(c, kt) for c in reversed(range(CHUNKS)) for kt in range(CT * c + CT)]
        NU = len(units)
        diag = [kt - CT * c if kt >= CT * c else None for c, kt in units]
        q0s = [0 if d is None else d * P for d in diag]
        PER_BANK = [len(range(i, NU * HG, SB)) for i in range(SB)]
        PER_SLOT = NU // 2
        DG = sum(d is not None for d in diag)
        LOADS = 2 * len(Q_PART) + 1

        items = []
        for h in range(HG):
            for qt in range(TT):
                keys = (qt + 1) * P
                if qt >= 2 * CT:
                    items.append((h, qt, 0, 2 * CH, False))
                    items.append((h, qt, 2 * CH, keys - 2 * CH, True))
                else:
                    items.append((h, qt, 0, keys, True))
        NI = len(items)
        assert NI % 2 == 0
        START, LAST = 1, 35
        cost = np.cumsum([i[3] + 70 for i in items])
        ucost = np.cumsum([0] * START + [CH - q for q in q0s[START:LAST]])
        plan = [[] for _ in range(NU)]
        for n, c in enumerate(cost):
            plan[int(np.searchsorted(ucost, (c - 1) / cost[-1] * ucost[-1]))].append(n)
        block = ctx.enter_context(nc.Block())

        @block.sync
        def _(sp):
            def load(g, r, q):
                rows, cols = bass.ds(g * GR, GR), slice(q * CH, (q + 1) * CH)
                for buf, side, parts in ((Ks, 1, K_PART), (Qs, 0, Q_PART)):
                    for i, p in enumerate(parts):
                        sp.dma_start(buf[r][i * HD:(i + 1) * HD, :, cols],
                                     qk_s[side, p, rows, cols].rearrange("(h d) n -> d h n", d=HD)
                                     ).then_inc(kv_in[r][q], 16)
                sp.dma_start(Vs[r][:, q * CT:(q + 1) * CT, :],
                             v_s[g, :, q * CT:(q + 1) * CT, :]).then_inc(kv_in[r][q], 16)

            def store_m(g, r):
                sp.wait_ge(mt_ok, ONE + g + 1)
                for i in range(MR):
                    sp.dma_start(Qs[r][PR + i:PR + i + 1, :, :].rearrange("o h n -> o (h n)"),
                                 nmT[i % 2 * HG * TT:(i % 2 + 1) * HG * TT, i // 2, :]).then_inc(m_in[r], 16)

            for r in range(2):
                for q in range(CHUNKS):
                    load(r, r, q)
            store_m(0, 0)

            def body(j, last):
                for r in range(2):
                    g = 2 * j + r
                    for n in range(CHUNKS):
                        i, use = n % 2, 2 * g + n // 2
                        if n == CHUNKS - 1 and not (last and r == 1):
                            store_m(g + 1, 1 - r)
                        sp.wait_ge(o_norm[i], ONE + use + 1)
                        for h in range(HG):
                            sp.dma_start(aT[r * GR + h * HD:r * GR + (h + 1) * HD, bass.ds(j, 1),
                                            (CHUNKS - 1 - n) * CH:(CHUNKS - n) * CH].rearrange("p o n -> p (o n)"),
                                         on[i][h * VW:h * VW + HD, :]).then_inc(o_stored[i], 16)
                        if not last:
                            load(g + 2, r, CHUNKS - 1 - n)

            with sp.Fori(0, GROUPS // 2 - 1) as j:
                body(j, False)
            body(GROUPS // 2 - 1, True)
            for i in range(2):
                sp.wait_ge(o_stored[i], ONE + 16 * HG * 2 * GROUPS)

        @block.gpsimd
        def _(pool):
            for every in sems:
                pool.sem_inc(every, ONE)
            nc.gpsimd.memset(identb[:, :], 0.0).then_inc(pool_b, 1)
            nc.gpsimd.memset(causal[:, :], 0.0).then_inc(pool_b, 1)
            pool.wait_ge(pool_b, ONE + 2)
            nc.gpsimd.affine_select(out=identb[:, :], in_=identb[:, :], compare_op=ALU.not_equal, fill=1.0, base=0,
                                    pattern=[[-1, P]], channel_multiplier=1).then_inc(const, 1)
            tri = causal[:, 2 * CH - P:2 * CH]
            nc.gpsimd.affine_select(out=tri, in_=tri, compare_op=ALU.is_ge, fill=LOW, base=0,
                                    pattern=[[-1, P]], channel_multiplier=1).then_inc(const, 1)
            nc.gpsimd.memset(blk[:, :, :], LOW).then_inc(const, 1)
            nc.gpsimd.memset(nmp[:, MR, :], 0.0).then_inc(const, 1)

            def body(j):
                for r in range(2):
                    g = 2 * j + r
                    nd = 0
                    for u, (c, kt) in enumerate(units):
                        if diag[u] is not None:
                            for h in range(HG):
                                n = u * HG + h
                                pool.wait_ge(s_read[n % SB], ONE + PER_BANK[n % SB] * g + n // SB + 1)
                            v = probs[u % 2][:, :, q0s[u]:q0s[u] + P]
                            pool.sem_inc(carrier, 1)
                            nc.gpsimd.affine_select(out=v, in_=v, compare_op=ALU.is_ge, fill=0.0, base=0,
                                                    pattern=[[0, HG], [1, P]], channel_multiplier=-1
                                                    ).then_inc(masked, 1)
                        if kt == CT * c + CT - 1:
                            i, use = nd % 2, 2 * g + nd // 2
                            nd += 1
                            pool.wait_ge(rs_ok[i], ONE + use + 1)
                            pool.wait_ge(o_stored[i], ONE + 16 * HG * use)
                            nc.gpsimd.tensor_tensor(on[i][:, :], ot[i][:, :], rsum[i][:, :], ALU.mult
                                                    ).then_inc(o_norm[i], 1)

            with pool.Fori(0, GROUPS // 2) as j:
                body(j)

        @block.scalar
        def _(act):
            def body(j):
                for r in range(2):
                    g = 2 * j + r

                    def copy_out(nd, u):
                        i, use = nd % 2, 2 * g + nd // 2
                        act.wait_ge(pv_ok[u % 2], ONE + PER_SLOT * g + u // 2 + 1)
                        act.wait_ge(o_norm[i], ONE + use)
                        nc.scalar.copy(ot[i][:, :], psO[:, :]).then_inc(o_copied, 1)

                    nd = 0
                    for u, (c, kt) in enumerate(units):
                        q0 = q0s[u]
                        act.wait_ge(pv_ok[u % 2], ONE + PER_SLOT * g + u // 2)
                        for h in range(HG):
                            n = u * HG + h
                            act.wait_ge(s_ps, ONE + NU * HG * g + n + 1)
                            nc.scalar.activation(probs[u % 2][:, h, q0:CH], psS[:, n % SB, q0:CH], ACT.Exp,
                                                 scale=SCALE).then_inc(s_read[n % SB], 1)
                            if u > 0 and h == 3 and units[u - 1][1] == CT * units[u - 1][0] + CT - 1:
                                copy_out(nd, u - 1)
                                nd += 1
                    copy_out(nd, NU - 1)

            with act.Fori(0, GROUPS // 2) as j:
                body(j)

        @block.vector
        def _(dve):
            ROWSUM = [16 + i % 16 for i in range(32)]

            def first(g, n):
                h, qt, k0, keys, last = items[n]
                slot = n % 2
                dve.wait_ge(first_ps[slot], ONE + NI // 2 * g + n // 2 + 1)
                m = blk[:, h * TT + qt, int(last):int(last) + 1]
                if last:
                    dve.sem_inc(carrier, 1)
                    ins = nc.vector.tensor_tensor_reduce(trash[:, slot, 0:keys], psP[:, slot, 0:keys],
                                                         causal[:, 2 * CH - keys:2 * CH], 1.0, LOW,
                                                         ALU.add, ALU.max, m)
                else:
                    ins = nc.vector.tensor_reduce(m, psP[:, slot, 0:keys], AX.X, ALU.max)
                ins.then_inc(first_ok[slot], 1)

            MS = 5

            def parts(g):
                for i in range(2):
                    dve.wait_ge(first_ok[i], ONE + NI // 2 * (g + 1))
                nc.vector.tensor_reduce(nm[:, :], blk[:, :, :], AX.X, ALU.max, negate=True).then_inc(m_step, 1)
                dve.wait_ge(m_step, ONE + MS * g + 1)
                nc.vector.tensor_copy(nmp[:, 0, :], nm[:, :]).then_inc(m_step, 1)
                dve.wait_ge(m_step, ONE + MS * g + 2)
                nc.vector.tensor_tensor(nm[:, :], nm[:, :], nmp[:, 0, :], ALU.subtract).then_inc(m_step, 1)
                dve.wait_ge(m_step, ONE + MS * g + 3)
                nc.vector.tensor_copy(nmp[:, 1, :], nm[:, :]).then_inc(m_step, 1)
                dve.wait_ge(m_step, ONE + MS * g + 4)
                nc.vector.tensor_tensor(nmp[:, 2, :], nm[:, :], nmp[:, 1, :], ALU.subtract).then_inc(m_step, 1)

            def rows(g):
                dve.wait_ge(mt_ps, ONE + g + 1)
                nc.vector.tensor_copy(nmT[:, :, :], psP[:, 0, :].bitcast(BF16)[:, 0:2 * P]
                                      .rearrange("p (m q) -> p m q", m=2)).then_inc(mt_ok, 1)

            def recip(g, nd):
                i, use = nd % 2, 2 * g + nd // 2
                dve.wait_ge(o_copied, ONE + CHUNKS * g + nd + 1)
                dve.wait_ge(o_norm[i], ONE + use)
                dve.sem_inc(carrier, 1)
                nc.vector.stream_shuffle(rsum[i][:, :], ot[i][:, :], ROWSUM).then_inc(r_step, 1)
                dve.wait_ge(r_step, ONE + CHUNKS * g + nd + 1)
                nc.vector.reciprocal(rsum[i][:, :], rsum[i][:, :]).then_inc(rs_ok[i], 1)

            for r in range(2):
                nc.vector.memset(Ks[r][PR:PR + MR, :, :], 1.0).then_inc(const, 1)
            dve.wait_ge(const, ONE + 6)
            for n in range(NI):
                first(0, n)
            parts(0)
            rows(0)

            def body(j, last):
                for r in range(2):
                    g = 2 * j + r
                    more = not (last and r == 1)
                    nd = 0
                    for u, (c, kt) in enumerate(units):
                        if more:
                            for n in plan[u]:
                                first(g + 1, n)
                            if u == LAST:
                                parts(g + 1)
                            if u == LAST + 2:
                                dve.wait_ge(m_in[r], ONE + 16 * MR * (j + 1))
                                rows(g + 1)
                        if u >= 2 and units[u - 2][1] == CT * units[u - 2][0] + CT - 1:
                            recip(g, nd)
                            nd += 1
                    recip(g, nd)

            with dve.Fori(0, GROUPS // 2 - 1) as j:
                body(j, False)
            body(GROUPS // 2 - 1, True)

        @block.tensor
        def _(pe):
            def first(g, r, n):
                h, qt, k0, keys, last = items[n]
                slot = n % 2
                pe.wait_ge(first_ok[slot], ONE + NI // 2 * g + n // 2)
                for k in range(0, keys, CH):
                    w = min(CH, keys - k)
                    ins = pe.matmul(psP[:, slot, k:k + w], Qs[r][0:PR, h, qt * P:(qt + 1) * P],
                                    Ks[r][0:PR, h, k0 + k:k0 + k + w], start=True, stop=True)
                ins.then_inc(first_ps[slot], 1)

            def rows(g):
                pe.wait_ge(m_step, ONE + 5 * g + 5)
                dst = psP[:, 0, :].bitcast(BF16)
                for i in range(2):
                    ins = pe.transpose(dst[:, i * P:(i + 1) * P],
                                       nmp[:, 2 * i:2 * i + 2, :].rearrange("p m n -> p (m n)"), identb[:, :])
                ins.then_inc(mt_ps, 1)

            def arrived(j, r):
                for q in range(CHUNKS):
                    pe.wait_ge(kv_in[r][q], ONE + 16 * LOADS * (j + 1))

            pe.wait_ge(const, ONE + 6)
            arrived(0, 0)
            for n in range(NI):
                first(0, 0, n)
            rows(0)

            def body(j, last):
                for r in range(2):
                    g = 2 * j + r
                    more = not (last and r == 1)

                    def scores(u, h):
                        n, q0 = u * HG + h, q0s[u]
                        c, kt = units[u]
                        pe.wait_ge(s_read[n % SB], ONE + PER_BANK[n % SB] * g + n // SB)
                        pe.matmul(psS[:, n % SB, q0:CH], Ks[r][:, h, kt * P:(kt + 1) * P],
                                  Qs[r][:, h, c * CH + q0:(c + 1) * CH], start=True, stop=True).then_inc(s_ps, 1)

                    nds = [0]

                    def pv(u):
                        c, kt = units[u]
                        q0, end = q0s[u], kt == CT * c + CT - 1
                        if diag[u] is None:
                            for h in range(HG):
                                n = u * HG + h
                                pe.wait_ge(s_read[n % SB], ONE + PER_BANK[n % SB] * g + n // SB + 1)
                        else:
                            pe.wait_ge(masked, ONE + DG * g + sum(d is not None for d in diag[:u]) + 1)
                        if kt == 0:
                            pe.wait_ge(o_copied, ONE + CHUNKS * g + (CHUNKS - 1 - c))
                        for h in range(HG):
                            ins = pe.matmul(psO[h * VW:(h + 1) * VW, q0:CH], Vs[r][:, kt, h * VW:(h + 1) * VW],
                                            probs[u % 2][:, h, q0:CH], start=(kt == 0), stop=end,
                                            tile_position=(0, h * VW))
                        ins.then_inc(pv_ok[u % 2], 1)

                    pe.wait_ge(m_in[r], ONE + 16 * MR * (j + 1))
                    for u in range(NU):
                        todo = list(plan[u]) if more else []
                        if u == START and more:
                            arrived(j + r, 1 - r)
                        scores(u, 0)
                        scores(u, 1)
                        if todo:
                            first(g + 1, 1 - r, todo.pop(0))
                        scores(u, 2)
                        if todo:
                            first(g + 1, 1 - r, todo.pop(0))
                        scores(u, 3)
                        if u > 0:
                            pv(u - 1)
                        while todo:
                            first(g + 1, 1 - r, todo.pop(0))
                        if more and u == LAST + 1:
                            rows(g + 1)
                    pv(NU - 1)

            with pe.Fori(0, GROUPS // 2 - 1) as j:
                body(j, False)
            body(GROUPS // 2 - 1, True)


def output(nc, wout, acc, aT, out):
    with ExitStack() as ctx:
        sem = lambda n: ctx.enter_context(nc.semaphore(n))
        wo = ctx.enter_context(nc.sbuf_tensor("wo", [P, KC, D], F32))
        ps = ctx.enter_context(nc.psum_tensor("ps", [P, 8, CH], F32))
        w_in = sem("wo_in")
        o_ps = sem("o_ps")
        o_add = sem("o_add")
        o_out = sem("o_out")
        block = ctx.enter_context(nc.Block())

        @block.sync
        def _(sp):
            sp.dma_start(wo[:, :, :], wout.rearrange("(k p) n -> p k n", p=P)).then_inc(w_in, 16)
            for c in range(TILES // CT):
                sp.wait_ge(o_add, CT * (c + 1))
                sp.dma_start(out[c // CHUNKS, c % CHUNKS * CH:(c % CHUNKS + 1) * CH, :]
                             .rearrange("(t p) d -> p t d", p=P), acc[:, c * CT:(c + 1) * CT, :]).then_inc(o_out, 16)
            sp.wait_ge(o_out, 16 * TILES // CT)

        @block.tensor
        def _(pe):
            pe.wait_ge(w_in, 16)
            for t in range(TILES):
                b, r = t // TT, t % TT
                if t >= 8:
                    pe.wait_ge(o_add, t - 7)
                for k in range(KC):
                    ins = pe.matmul(ps[:, t % 8, 0:D], aT[:, 2 * b + k, r * P:(r + 1) * P], wo[:, k, :],
                                    start=(k == 0), stop=(k == KC - 1))
                ins.then_inc(o_ps, 1)

        @block.vector
        def _(dve):
            for t in range(TILES):
                dve.wait_ge(o_ps, t + 1)
                nc.vector.tensor_tensor(acc[:, t, :], ps[:, t % 8, 0:D], acc[:, t, :], ALU.add).then_inc(o_add, 1)


def build(nc, x, wqk, wvg, wout, bout, gb, we, be, cos, sin, out):
    qk_s = nc.dram_tensor("qk_scratch", [2, 3, B * D, N], BF16, kind="Internal").ap()
    v_s = nc.dram_tensor("v_scratch", [GROUPS, P, TT, HG * VW], F32, kind="Internal").ap()
    with nc.sbuf_tensor("acc", [P, TILES, D], F32) as acc:
        project(nc, x, wqk, wvg, we, be, bout, gb, cos, sin, qk_s, v_s, acc)
        with nc.sbuf_tensor("aT", [P, B * KC, N], F32) as aT:
            attend(nc, qk_s, v_s, aT)
            output(nc, wout, acc, aT, out)


def rotary_tables():
    inv = (1.0 / np.float32(10000.0) ** (np.arange(0, HD, 2, dtype=np.float32) / np.float32(HD))).astype(np.float32)
    f = np.arange(N, dtype=np.float32)[None, :] * np.tile(np.repeat(inv, 2), P // HD)[:, None]
    sign = np.where(np.arange(P) % 2 == 0, -1.0, 1.0).astype(np.float32)[:, None]
    return np.cos(f).astype(np.float32), (np.sin(f) * sign).astype(np.float32)


def kernel(L0_attn_X, L0_attn_Wqkv, L0_attn_Wout, L0_attn_bout, L0_ffn_gate_w, L0_ffn_gate_b, L0_ffn_expert_w,
           L0_ffn_expert_b):
    import concourse.bacc as bacc
    from concourse.bass_utils import run_bass_kernel_spmd

    wqkv = np.asarray(L0_attn_Wqkv)
    cos, sin = rotary_tables()
    arrays = {
        "x": np.ascontiguousarray(L0_attn_X),
        "wqk": np.ascontiguousarray(wqkv[:, :2 * D]),
        "wvg": np.ascontiguousarray(np.concatenate([wqkv[:, 2 * D:], np.asarray(L0_ffn_gate_w).T], axis=1)),
        "wout": np.ascontiguousarray(L0_attn_Wout),
        "bout": np.asarray(L0_attn_bout).reshape(1, D),
        "gb": np.asarray(L0_ffn_gate_b).reshape(1, GATES),
        "we": np.ascontiguousarray(L0_ffn_expert_w),
        "be": np.ascontiguousarray(L0_ffn_expert_b),
        "cos": cos,
        "sin": sin,
    }
    nc = bacc.Bacc("TRN2", target_bir_lowering=False, num_devices=1)
    args = [nc.dram_tensor(n, a.shape, mybir.dt.from_np(a.dtype), kind="ExternalInput").ap()
            for n, a in arrays.items()]
    out = nc.dram_tensor("out", (B, N, D), F32, kind="ExternalOutput").ap()
    build(nc, *args, out)
    r = run_bass_kernel_spmd(nc, [arrays], core_ids=[0])
    return r.results[0]["out"]
```

```python
from contextlib import ExitStack

import numpy as np

import concourse.bass as bass
from concourse import mybir

ALU = mybir.AluOpType
ACT = mybir.ActivationFunctionType
AX = mybir.AxisListType
F32 = mybir.dt.float32
BF16 = mybir.dt.bfloat16
U32 = mybir.dt.uint32

P = 128
B, N, D = 2, 2048, 256
HEADS, HD = 16, 16
EXPERTS, GATES = 8, 10
EPS = 1e-5
SCALE = HD ** -0.5
KC = D // P
TT = N // P
TILES = B * TT
CH = 512
CT = CH // P
CHUNKS = N // CH
QKT = 2 * D // P
HG = 4
GROUPS = B * HEADS // HG
GR = HG * HD
VW = 32
BLOCKS = ((3, 0), (2, 1), (1, 2))
PR = sum(n for n, _ in BLOCKS) * HD
MR = 3
LOW = -3.0e38
ONE = 1


def project(nc, x, wqk, wvg, we, be, bout, gb, cos, sin, qk_s, v_s, acc):
    with ExitStack() as ctx:
        sb = lambda n, s, d=F32: ctx.enter_context(nc.sbuf_tensor(n, s, d))
        sems = []

        def sem(n):
            sems.append(ctx.enter_context(nc.semaphore(n)))
            return sems[-1]

        pair = lambda n: [sem(f"{n}{i}") for i in range(2)]

        ident = sb("ident", [P, P])
        wqk_sb = sb("wqk_sb", [P, KC, 2 * D])
        wvg_sb = sb("wvg_sb", [P, KC, D + GATES])
        we_sb = sb("we_sb", [P, KC, EXPERTS * D])
        be_sb = sb("be_sb", [EXPERTS + 1, D])
        gb_sb = sb("gb_sb", [P, GATES])
        trig = sb("trig", [P, 2, CH])
        iota = sb("iota", [P, GATES])
        eps = sb("eps", [P, 1])
        xs = [sb(f"xs{i}", [P, CT, D]) for i in range(2)]
        xn = [sb(f"xn{i}", [P, CT, D]) for i in range(2)]
        xnT = [sb(f"xnT{i}", [P, KC, CH]) for i in range(2)]
        stat = sb("stat", [P, CT, 6])
        mv = sb("mv", [P, CT, 2])
        std = sb("std", [P, CT])
        rstd = sb("rstd", [P, CT])
        vst = [sb(f"vst{i}", [P, CT, HEADS, VW]) for i in range(2)]
        lg = [sb(f"lg{i}", [P, CT, GATES]) for i in range(2)]
        gl = sb("gl", [P, CT, GATES])
        ge = sb("ge", [P, CT, GATES])
        gp = sb("gp", [P, CT, GATES])
        gm = sb("gm", [P, CT])
        gr = sb("gr", [P, CT])
        top = sb("top", [P, CT, 8])
        topi = sb("topi", [P, CT, 8], U32)
        topf = sb("topf", [P, CT, 2])
        hot = sb("hot", [P, 2, CT, GATES])
        cw = sb("cw", [P, CT, EXPERTS])
        den = sb("den", [P, CT])
        dez = sb("dez", [P, CT])
        c9 = [sb(f"c9{i}", [P, CT, EXPERTS + 1]) for i in range(2)]
        c9T = sb("c9T", [EXPERTS + 1, CH])
        odd = [sb(f"odd{i}", [P, D]) for i in range(2)]
        rot = [sb(f"rot{i}", [P, CH]) for i in range(QKT)]
        swp = [sb(f"swp{i}", [P, CH]) for i in range(QKT)]
        part = [sb(f"part{i}", [P, 3, CH], BF16) for i in range(QKT)]

        psT = ctx.enter_context(nc.psum_tensor("psT", [P, 2, CH], F32))
        psQ = ctx.enter_context(nc.psum_tensor("psQ", [P, 2, CH], F32))
        psM = ctx.enter_context(nc.psum_tensor("psM", [P, 2, CH], F32))
        psC = ctx.enter_context(nc.psum_tensor("psC", [P, CH], F32))
        psB = ctx.enter_context(nc.psum_tensor("psB", [P, D], F32))

        x_in = pair("x_in")
        acc_stored = pair("acc_stored")
        w_in = sem("w_in")
        w2_in = sem("w2_in")
        trig_in = sem("trig_in")
        const = sem("const")
        vcol = sem("vcol")
        stats = sem("stats")
        std_ok = sem("std_ok")
        xn_ok = sem("xn_ok")
        xT_ps = sem("xT_ps")
        xT_ok = sem("xT_ok")
        vg_ps = sem("vg_ps")
        vg_ok = sem("vg_ok")
        v_stored = pair("v_stored")
        gate_in = sem("gate_in")
        gate_e = sem("gate_e")
        gate_c = sem("gate_c")
        qk_ps = sem("qk_ps")
        each = lambda n: [sem(f"{n}{k}") for k in range(QKT)]
        rope_ok = each("rope_ok")
        sum_ok = each("sum_ok")
        high_ok = each("high_ok")
        rest_ok = each("rest_ok")
        mid_ok = each("mid_ok")
        split_ok = each("split_ok")
        part_stored = each("part_stored")
        moe_ps = sem("moe_ps")
        moe_read = pair("moe_read")
        cT_ps = sem("cT_ps")
        cT_ok = sem("cT_ok")
        bias_ps = sem("bias_ps")
        bias_read = sem("bias_read")
        acc_ok = sem("acc_ok")
        carrier = sem("carrier")
        dve_step = sem("dve_step")
        pool_step = sem("pool_step")

        STORES = 3 * P // GR
        NB = B
        block = ctx.enter_context(nc.Block())

        @block.sync
        def _(sp):
            def load_x(j, b):
                sp.dma_start(xs[b][:, :, :],
                             x[b, bass.ds(j * CH, CH), :].rearrange("(t p) d -> p t d", p=P)).then_inc(x_in[b], 16)

            def load_trig(j):
                sp.dma_start(trig[:, 0, :], cos[:, bass.ds(j * CH, CH)]).then_inc(trig_in, 16)
                sp.dma_start(trig[:, 1, :], sin[:, bass.ds(j * CH, CH)]).then_inc(trig_in, 16)

            load_x(0, 0)
            sp.dma_start(wvg_sb[:, :, :], wvg.rearrange("(k p) n -> p k n", p=P)).then_inc(w_in, 16)
            sp.dma_start(wqk_sb[:, :, :], wqk.rearrange("(k p) n -> p k n", p=P)).then_inc(w_in, 16)
            sp.dma_start(gb_sb[:, :], gb.partition_broadcast(P)).then_inc(w_in, 16)
            load_trig(0)
            load_x(0, 1)
            for e in range(EXPERTS):
                sp.dma_start(we_sb[:, :, e * D:(e + 1) * D],
                             we[e].rearrange("(k p) n -> p k n", p=P)).then_inc(w2_in, 16)
            sp.dma_start(be_sb[0:EXPERTS, :], be).then_inc(w2_in, 16)
            sp.dma_start(be_sb[EXPERTS:EXPERTS + 1, :], bout).then_inc(w2_in, 16)

            def body(j, last):
                for b in range(NB):
                    for k in range(QKT):
                        sp.wait_ge(split_ok[k], ONE + (2 * j + b) + 1)
                        for i in range(P // GR):
                            for p in range(3):
                                dst = qk_s[k // 2, b * (HEADS // HG) + k % 2 * (P // GR) + i, p, :, bass.ds(j, 1), :, :]
                                sp.dma_start(dst.rearrange("d o h n -> h d (o n)"),
                                             part[k][i * GR:(i + 1) * GR, p, :]).then_inc(part_stored[k], 16)
                    sp.wait_ge(vg_ok, ONE + (2 * j + b) * CT + CT)
                    for h in range(HEADS // HG):
                        sp.dma_start(v_s[b * (HEADS // HG) + h, :, bass.ds(j * CT, CT), :],
                                     vst[b][:, :, h * HG:(h + 1) * HG, :].rearrange("p t h w -> p t (h w)")
                                     ).then_inc(v_stored[b], 16)
                    if b == 1 and not last:
                        for k in range(QKT):
                            sp.wait_ge(rope_ok[k], ONE + 2 * j + 2)
                            sp.wait_ge(sum_ok[k], ONE + 2 * j + 2)
                        sp.sem_inc(carrier, 1)
                        load_trig(j + 1)
                    sp.wait_ge(acc_ok, ONE + (2 * j + b) * CT + CT)
                    sp.dma_start(acc[:, bass.ds(j * CT + b * TT, CT), :], xs[b][:, :, :]).then_inc(acc_stored[b], 16)
                    if not last:
                        sp.wait_ge(acc_stored[b], ONE + 16 * j + 16)
                        load_x(j + 1, b)

            with sp.Fori(0, CHUNKS - 1) as j:
                body(j, False)
            body(CHUNKS - 1, True)
            for b in range(2):
                sp.wait_ge(acc_stored[b], ONE + 16 * CHUNKS)
                sp.wait_ge(v_stored[b], ONE + 16 * (HEADS // HG) * CHUNKS)
            for k in range(QKT):
                sp.wait_ge(part_stored[k], ONE + 16 * STORES * NB * CHUNKS)

        @block.gpsimd
        def _(pool):
            for every in sems:
                pool.sem_inc(every, ONE)
            steps = [0]

            def step(ins):
                steps[0] += 1
                return ins.then_inc(pool_step, 1)

            step(nc.gpsimd.memset(ident[:, :], 0.0))
            pool.wait_ge(pool_step, ONE + 1)
            nc.gpsimd.affine_select(out=ident[:, :], in_=ident[:, :], compare_op=ALU.not_equal, fill=1.0, base=0,
                                    pattern=[[-1, P]], channel_multiplier=1).then_inc(const, 1)
            nc.gpsimd.iota(iota[:, :], pattern=[[1, GATES]], base=0, channel_multiplier=0,
                           allow_small_or_imprecise_dtypes=True).then_inc(const, 1)
            nc.gpsimd.memset(eps[:, :], EPS).then_inc(const, 1)
            for b in range(NB):
                nc.gpsimd.memset(vst[b][:, :, :, :], 1.0).then_inc(const, 1)
                nc.gpsimd.memset(c9[b][:, :, :], 1.0).then_inc(const, 1)

            def body(j):
                pool.wait_ge(trig_in, ONE + 32 * j + 32)
                for b in range(NB):
                    s = 2 * j + b
                    for k in range(QKT):
                        pool.wait_ge(rope_ok[k], ONE + s + 1)
                        step(nc.gpsimd.tensor_tensor(swp[k][:, :], swp[k][:, :], trig[:, 1, :], ALU.mult))
                        pool.wait_ge(pool_step, ONE + 1 + QKT * s + k + 1)
                        nc.gpsimd.tensor_tensor(rot[k][:, :], rot[k][:, :], swp[k][:, :], ALU.add
                                                ).then_inc(sum_ok[k], 1)
                    for k in range(QKT):
                        pool.wait_ge(high_ok[k], ONE + s + 1)
                        nc.gpsimd.tensor_tensor(rot[k][:, :], rot[k][:, :], part[k][:, 0, :], ALU.subtract
                                                ).then_inc(rest_ok[k], 1)
                    for k in range(QKT):
                        pool.wait_ge(mid_ok[k], ONE + s + 1)
                        nc.gpsimd.tensor_tensor(part[k][:, 2, :], rot[k][:, :], part[k][:, 1, :], ALU.subtract
                                                ).then_inc(split_ok[k], 1)

            with pool.Fori(0, CHUNKS) as j:
                body(j)

        @block.scalar
        def _(act):
            def deviation(s):
                act.wait_ge(stats, ONE + s + 1)
                nc.scalar.activation(std[:, :], mv[:, :, 1], ACT.Sqrt, bias=eps[:, :]).then_inc(std_ok, 1)

            def copy_xT(s, b):
                for k in range(KC):
                    act.wait_ge(xT_ps, ONE + KC * s + k + 1)
                    nc.scalar.copy(xnT[b][:, k, :], psT[:, k, :]).then_inc(xT_ok, 1)

            act.wait_ge(const, ONE + 7)
            deviation(0)
            copy_xT(0, 0)

            def body(j, last):
                for b in range(NB):
                    s = 2 * j + b
                    act.wait_ge(v_stored[b], ONE + 16 * (HEADS // HG) * j)
                    for t in range(CT):
                        act.wait_ge(vg_ps, ONE + CT * s + t + 1)
                        nc.scalar.copy(vst[b][:, t, :, 0:HD],
                                       psT[:, t % 2, 0:D].rearrange("p (h d) -> p h d", d=HD)).then_inc(vcol, 1)
                        nc.scalar.copy(lg[b][:, t, :], psT[:, t % 2, D:D + GATES]).then_inc(vg_ok, 1)
                    act.wait_ge(gate_in, ONE + s + 1)
                    nc.scalar.activation(ge[:, :, :], gl[:, :, :], ACT.Exp).then_inc(gate_e, 1)
                    for k in range(QKT):
                        act.wait_ge(sum_ok[k], ONE + s + 1)
                        act.wait_ge(part_stored[k], ONE + 16 * STORES * s)
                        nc.scalar.copy(part[k][:, 0, :], rot[k][:, :]).then_inc(high_ok[k], 1)
                    for k in range(QKT):
                        act.wait_ge(rest_ok[k], ONE + s + 1)
                        nc.scalar.copy(part[k][:, 1, :], rot[k][:, :]).then_inc(mid_ok[k], 1)
                    if not (last and b == 1):
                        deviation(s + 1)
                        copy_xT(s + 1, 1 - b)

            with act.Fori(0, CHUNKS - 1) as j:
                body(j, False)
            body(CHUNKS - 1, True)

        @block.vector
        def _(dve):
            n = [0]

            def step(ins):
                n[0] += 1
                return ins.then_inc(dve_step, 1)

            def norm_a(j, b):
                dve.wait_ge(x_in[b], ONE + 16 * j + 16)
                for t in range(CT):
                    step(nc.vector.bn_stats(stat[:, t, :], xs[b][:, t, :]))

            def norm_b(base):
                for t in range(CT):
                    dve.wait_ge(dve_step, ONE + base + t + 1)
                    dve.sem_inc(carrier, 1)
                    ins = nc.vector.bn_aggr(mv[:, t, :], stat[:, t, :])
                ins.then_inc(stats, 1)

            def norm_c(s, b, base, before=None):
                dve.wait_ge(std_ok, ONE + s + 1)
                step(nc.vector.reciprocal(rstd[:, :], std[:, :]))
                dve.wait_ge(dve_step, ONE + base + 1)
                if before is not None:
                    dve.wait_ge(xT_ps, ONE + KC * before)
                for t in range(CT):
                    ins = nc.vector.tensor_scalar(xn[b][:, t, :], xs[b][:, t, :], mv[:, t, 0:1], rstd[:, t:t + 1],
                                                  ALU.subtract, ALU.mult)
                ins.then_inc(xn_ok, 1)

            SWAP = [i ^ 1 for i in range(32)]

            def rope(s, k):
                dve.wait_ge(qk_ps, ONE + QKT * s + k + 1)
                dve.wait_ge(split_ok[k], ONE + s)
                dve.sem_inc(carrier, 1)
                nc.vector.stream_shuffle(swp[k][:, :], psQ[:, k % 2, :], SWAP)
                nc.vector.tensor_tensor(rot[k][:, :], psQ[:, k % 2, :], trig[:, 0, :], ALU.mult
                                        ).then_inc(rope_ok[k], 1)

            def wide(a):
                return a.unsqueeze(2).to_broadcast([P, CT, GATES])

            def gates_a(s, b, base):
                dve.wait_ge(vg_ok, ONE + CT * s + CT)
                step(nc.vector.tensor_tensor(gl[:, :, :], lg[b][:, :, :],
                                             gb_sb[:, :].unsqueeze(1).to_broadcast([P, CT, GATES]), ALU.add))
                dve.wait_ge(dve_step, ONE + base + 1)
                step(nc.vector.tensor_reduce(gm[:, :], gl[:, :, :], AX.X, ALU.max))
                dve.wait_ge(dve_step, ONE + base + 2)
                nc.vector.tensor_tensor(gl[:, :, :], gl[:, :, :], wide(gm[:, :]), ALU.subtract).then_inc(gate_in, 1)

            def gates_b(s, b, base):
                dve.wait_ge(gate_e, ONE + s + 1)
                step(nc.vector.tensor_reduce(gr[:, :], ge[:, :, :], AX.X, ALU.add))
                dve.wait_ge(dve_step, ONE + base + 1)
                step(nc.vector.reciprocal(gr[:, :], gr[:, :]))
                dve.wait_ge(dve_step, ONE + base + 2)
                step(nc.vector.tensor_tensor(gp[:, :, :], ge[:, :, :], wide(gr[:, :]), ALU.mult))
                dve.wait_ge(dve_step, ONE + base + 3)
                for t in range(CT):
                    dve.sem_inc(carrier, 1)
                    step(nc.vector.max(top[:, t, :], gp[:, t, :]))
                for t in range(CT):
                    dve.wait_ge(dve_step, ONE + base + 4 + t)
                    dve.sem_inc(carrier, 1)
                    step(nc.vector.max_index(topi[:, t, :], top[:, t, :], gp[:, t, :]))
                dve.wait_ge(dve_step, ONE + base + 11)
                step(nc.vector.tensor_copy(topf[:, :, :], topi[:, :, 0:2]))
                dve.wait_ge(dve_step, ONE + base + 12)
                for i in range(2):
                    step(nc.vector.tensor_tensor(hot[:, i, :, :], iota[:, :].unsqueeze(1).to_broadcast([P, CT, GATES]),
                                                 topf[:, :, i:i + 1].to_broadcast([P, CT, GATES]), ALU.is_equal))
                dve.wait_ge(dve_step, ONE + base + 14)
                step(nc.vector.tensor_tensor(hot[:, 0, :, :], hot[:, 0, :, :], hot[:, 1, :, :], ALU.add))
                dve.wait_ge(dve_step, ONE + base + 15)
                step(nc.vector.tensor_tensor(cw[:, :, :], gp[:, :, 0:EXPERTS], hot[:, 0, :, 0:EXPERTS], ALU.mult))
                dve.wait_ge(dve_step, ONE + base + 16)
                step(nc.vector.tensor_reduce(den[:, :], cw[:, :, :], AX.X, ALU.add))
                dve.wait_ge(dve_step, ONE + base + 17)
                step(nc.vector.tensor_single_scalar(dez[:, :], den[:, :], 0.0, ALU.is_le))
                dve.wait_ge(dve_step, ONE + base + 18)
                step(nc.vector.tensor_tensor(den[:, :], den[:, :], dez[:, :], ALU.add))
                dve.wait_ge(dve_step, ONE + base + 19)
                step(nc.vector.reciprocal(den[:, :], den[:, :]))
                dve.wait_ge(dve_step, ONE + base + 20)
                nc.vector.tensor_tensor(c9[b][:, :, 0:EXPERTS], cw[:, :, :],
                                        den[:, :].unsqueeze(2).to_broadcast([P, CT, EXPERTS]), ALU.mult
                                        ).then_inc(gate_c, 1)

            def combine(s, b, t, base):
                dve.wait_ge(gate_c, ONE + s + 1)
                for n4 in range(EXPERTS // 2):
                    slot, uses = n4 % 2, (EXPERTS // 4) * (CT * s + t)
                    dve.wait_ge(moe_ps, ONE + (EXPERTS // 2) * (CT * s + t) + n4 + 1)
                    e = 2 * n4
                    if n4 > 0:
                        dve.wait_ge(dve_step, ONE + base + n4)
                    step(nc.vector.scalar_tensor_tensor(out=xs[b][:, t, :], in0=psM[:, slot, 0:D],
                                                        scalar=c9[b][:, t, e:e + 1], in1=xs[b][:, t, :],
                                                        op0=ALU.mult, op1=ALU.add))
                    if n4 == 0:
                        ins = nc.vector.tensor_scalar(odd[t % 2][:, :], psM[:, slot, D:2 * D],
                                                      c9[b][:, t, e + 1:e + 2], None, ALU.mult)
                    else:
                        dve.wait_ge(moe_read[1 - slot], ONE + uses + (n4 - 1) // 2 + 1)
                        ins = nc.vector.scalar_tensor_tensor(out=odd[t % 2][:, :], in0=psM[:, slot, D:2 * D],
                                                             scalar=c9[b][:, t, e + 1:e + 2], in1=odd[t % 2][:, :],
                                                             op0=ALU.mult, op1=ALU.add)
                    ins.then_inc(moe_read[slot], 1)
                dve.wait_ge(bias_ps, ONE + CT * s + t + 1)
                dve.wait_ge(moe_read[1], ONE + uses + EXPERTS // 4)
                nc.vector.tensor_tensor(odd[t % 2][:, :], psB[:, :], odd[t % 2][:, :], ALU.add
                                        ).then_inc(bias_read, 1)
                dve.wait_ge(dve_step, ONE + base + EXPERTS // 2)
                dve.wait_ge(bias_read, ONE + CT * s + t + 1)
                nc.vector.tensor_tensor(xs[b][:, t, :], xs[b][:, t, :], odd[t % 2][:, :], ALU.add).then_inc(acc_ok, 1)

            GA, GB, CB, NA, NCC = 2, 20, EXPERTS // 2, CT, 1
            FIRST = NA + NCC
            EACH = GA + GB + CT * CB + NA + NCC

            dve.wait_ge(const, ONE + 7)
            dve.wait_ge(w_in, ONE + 48)
            norm_a(0, 0)
            norm_b(0)
            norm_c(0, 0, NA)

            def body(j, last):
                dve.wait_ge(trig_in, ONE + 32 * j + 32)
                for b in range(NB):
                    s = 2 * j + b
                    at = FIRST + EACH * s
                    more = not (last and b == 1)
                    gates_a(s, b, at)
                    rope(s, 0)
                    rope(s, 1)
                    gates_b(s, b, at + GA)
                    rope(s, 2)
                    rope(s, 3)
                    dve.wait_ge(cT_ps, ONE + s + 1)
                    nc.vector.tensor_copy(c9T[:, :], psC[0:EXPERTS + 1, :]).then_inc(cT_ok, 1)
                    at = at + GA + GB
                    if more:
                        norm_a(j + b, 1 - b)
                        norm_b(at)
                        at = at + NA
                    combine(s, b, 0, at)
                    at = at + CB
                    if more:
                        norm_c(s + 1, 1 - b, at, before=s)
                        at = at + NCC
                    for t in range(1, CT):
                        combine(s, b, t, at)
                        at = at + CB

            with dve.Fori(0, CHUNKS - 1) as j:
                body(j, False)
            body(CHUNKS - 1, True)

        @block.tensor
        def _(pe):
            def transposes(s, b):
                pe.wait_ge(xn_ok, ONE + s + 1)
                for k in range(KC):
                    for t in range(CT):
                        ins = pe.transpose(psT[:, k, t * P:(t + 1) * P], xn[b][:, t, k * P:(k + 1) * P], ident[:, :])
                    ins.then_inc(xT_ps, 1)

            pe.wait_ge(const, ONE + 7)
            transposes(0, 0)
            pe.wait_ge(w_in, ONE + 48)

            def body(j, last):
                for b in range(NB):
                    s = 2 * j + b
                    pe.wait_ge(xT_ok, ONE + KC * s + KC)
                    for t in range(CT):
                        if t >= 2:
                            pe.wait_ge(vg_ok, ONE + CT * s + t - 1)
                        for k in range(KC):
                            ins = pe.matmul(psT[:, t % 2, 0:D + GATES], xnT[b][:, k, t * P:(t + 1) * P],
                                            wvg_sb[:, k, :], start=(k == 0), stop=(k == KC - 1))
                        ins.then_inc(vg_ps, 1)
                    for q in range(QKT):
                        pe.wait_ge(rope_ok[(q - 2) % QKT], ONE + s + q // 2)
                        for k in range(KC):
                            ins = pe.matmul(psQ[:, q % 2, :], wqk_sb[:, k, q * P:(q + 1) * P], xnT[b][:, k, :],
                                            start=(k == 0), stop=(k == KC - 1))
                        ins.then_inc(qk_ps, 1)
                    if b == 0:
                        pe.wait_ge(w2_in, ONE + 16 * (EXPERTS + 2))
                    for t in range(CT):
                        for n4 in range(EXPERTS // 2):
                            pe.wait_ge(moe_read[n4 % 2], ONE + (EXPERTS // 4) * (CT * s + t) + n4 // 2)
                            for k in range(KC):
                                ins = pe.matmul(psM[:, n4 % 2, :], xnT[b][:, k, t * P:(t + 1) * P],
                                                we_sb[:, k, n4 * 2 * D:(n4 + 1) * 2 * D],
                                                start=(k == 0), stop=(k == KC - 1))
                            ins.then_inc(moe_ps, 1)
                            if t == 0 and n4 == 1:
                                pe.wait_ge(gate_c, ONE + s + 1)
                                pe.wait_ge(cT_ok, ONE + s)
                                for u in range(CT):
                                    ins = pe.transpose(psC[0:EXPERTS + 1, u * P:(u + 1) * P], c9[b][:, u, :],
                                                       ident[:, :])
                                ins.then_inc(cT_ps, 1)
                        if t == 0:
                            pe.wait_ge(cT_ok, ONE + s + 1)
                        pe.wait_ge(bias_read, ONE + CT * s + t)
                        pe.matmul(psB[:, :], c9T[:, t * P:(t + 1) * P], be_sb[:, :], start=True, stop=True
                                  ).then_inc(bias_ps, 1)
                        if t == 1 and not (last and b == 1):
                            transposes(s + 1, 1 - b)

            with pe.Fori(0, CHUNKS - 1) as j:
                body(j, False)
            body(CHUNKS - 1, True)


def attend(nc, qk_s, v_s, on):
    with ExitStack() as ctx:
        sb = lambda n, s, d=F32: ctx.enter_context(nc.sbuf_tensor(n, s, d))
        sems = []

        def sem(n):
            sems.append(ctx.enter_context(nc.semaphore(n)))
            return sems[-1]

        pair = lambda n: [sem(f"{n}{i}") for i in range(2)]
        quarters = lambda n: [[sem(f"{n}{i}{c}") for c in range(CHUNKS)] for i in range(2)]

        Qs = [sb(f"Qs{i}", [PR + MR, CHUNKS, HG, CH], BF16) for i in range(2)]
        Ks = [sb(f"Ks{i}", [PR + MR, CHUNKS, HG, CH], BF16) for i in range(2)]
        Vs = [sb(f"Vs{i}", [P, TT, HG * VW]) for i in range(2)]
        probs = [sb(f"probs{i}", [P, HG, CH]) for i in range(2)]
        causal = sb("causal", [P, 2 * CH], BF16)
        trash = sb("trash", [P, 2, 2 * CH], BF16)
        MQ = HG * CT
        blk = sb("blk", [P, CHUNKS * MQ, 2])
        nm = sb("nm", [P, MQ])
        nmp = sb("nmp", [P, P // MQ, MQ], BF16)
        nmT = [sb(f"nmT{i}", [MR * MQ, P], BF16) for i in range(2)]
        identb = sb("identb", [P, P], BF16)
        identf = sb("identf", [P, P])
        ot = [sb(f"ot{i}", [P, CH]) for i in range(2)]
        rs = sb("rs", [P, CT, HG])

        SB = 3
        psS = ctx.enter_context(nc.psum_tensor("psS", [P, SB, CH], F32))
        psP = ctx.enter_context(nc.psum_tensor("psP", [P, 2, 2 * CH], F32))
        psO = ctx.enter_context(nc.psum_tensor("psO", [P, CH], F32))

        kv_in = quarters("kv_in")
        m_in = quarters("m_in")
        const = sem("const_b")
        s_ps = sem("s_ps")
        s_read = [sem(f"s_read{i}") for i in range(SB)]
        masked = sem("masked")
        pv_ok = pair("pv_ok")
        o_copied = sem("o_copied")
        oT_ps = pair("oT_ps")
        r_ok = sem("r_ok")
        o_norm = sem("o_norm")
        first_ps = pair("first_ps")
        first_ok = pair("first_ok")
        m_step = sem("m_step")
        carrier = sem("carrier_b")
        pool_b = sem("pool_b")

        units = [(c, kt) for c in reversed(range(CHUNKS)) for kt in range(CT * c + CT)]
        NU = len(units)
        diag = [kt - CT * c if kt >= CT * c else None for c, kt in units]
        q0s = [0 if d is None else d * P for d in diag]
        ends = [u for u, (c, kt) in enumerate(units) if kt == CT * c + CT - 1]
        PER_BANK = [len(range(i, NU * HG, SB)) for i in range(SB)]
        PER_SLOT = NU // 2
        DG = sum(d is not None for d in diag)
        LOADS = 2 * len(BLOCKS) + 1

        items = []
        pending = None
        LATER = 4
        for c in reversed(range(CHUNKS)):
            chunk = []
            for h in range(HG):
                for qt in range(c * CT, c * CT + CT):
                    keys = (qt + 1) * P
                    if qt >= 2 * CT:
                        chunk.append((h, qt, 0, 2 * CH, False))
                        chunk.append((h, qt, 2 * CH, keys - 2 * CH, True))
                    else:
                        chunk.append((h, qt, 0, keys, True))
            if pending is not None:
                chunk.insert(LATER, ("m", pending))
            pending = c
            items += chunk
        items.append(("m", 0))
        last_of = {}
        for n, it in enumerate(items):
            if it[0] != "m":
                last_of[it[1] // CT] = n
        NI = len(items)
        assert NI % 2 == 0
        START = 3
        cost = np.cumsum([200 if i[0] == "m" else i[3] + 70 for i in items])
        ucost = np.cumsum([0] * START + [CH - q for q in q0s[START:]])
        plan = [[] for _ in range(NU)]
        for n, c in enumerate(cost):
            plan[int(np.searchsorted(ucost, (c - 1) / cost[-1] * ucost[-1]))].append(n)
        plan[NU - 1].remove(NI - 1)
        block = ctx.enter_context(nc.Block())

        def q_rows(r, h, qt):
            return Qs[r][0:PR, qt // CT, h, qt % CT * P:(qt % CT + 1) * P]

        @block.sync
        def _(sp):
            def load(g, r, c):
                row = 0
                for n, p in BLOCKS:
                    rows = slice(row, row + n * HD)
                    row += n * HD
                    sp.dma_start(Qs[r][rows, c, :, :].rearrange("r h n -> r (h n)"),
                                 qk_s[0, g, 0:n, :, c, :, :].rearrange("p d h n -> (p d) (h n)")
                                 ).then_inc(kv_in[r][c], 16)
                    src = qk_s[1, g, p, :, c, :, :].rearrange("d h n -> d (h n)")
                    sp.dma_start(Ks[r][rows, c, :, :].rearrange("r h n -> r (h n)"),
                                 src.unsqueeze(0).to_broadcast([n, HD, HG * CH])).then_inc(kv_in[r][c], 16)
                sp.dma_start(Vs[r][:, c * CT:(c + 1) * CT, :],
                             v_s[g, :, c * CT:(c + 1) * CT, :]).then_inc(kv_in[r][c], 16)

            def store_m(g, r, c):
                n = items.index(("m", c))
                sp.wait_ge(first_ok[n % 2], ONE + NI // 2 * g + n // 2 + 1)
                sp.dma_start(Qs[r][PR:PR + MR, c, :, :].rearrange("r h n -> r (h n)"),
                             nmT[c % 2][:, :]).then_inc(m_in[r][c], 16)

            for r in range(2):
                for c in reversed(range(CHUNKS)):
                    load(r, r, c)
            for c in reversed(range(CHUNKS)):
                store_m(0, 0, c)

            def body(j, last):
                for r in range(2):
                    g = 2 * j + r
                    for n, c in enumerate(reversed(range(CHUNKS))):
                        if not last:
                            u = ends[n]
                            sp.wait_ge(pv_ok[u % 2], ONE + PER_SLOT * g + u // 2 + 1)
                            sp.sem_inc(carrier, 1)
                            load(g + 2, r, c)
                        if not (last and r == 1):
                            store_m(g + 1, 1 - r, c)

            with sp.Fori(0, GROUPS // 2 - 1) as j:
                body(j, False)
            body(GROUPS // 2 - 1, True)

        @block.gpsimd
        def _(pool):
            for every in sems:
                pool.sem_inc(every, ONE)
            nc.gpsimd.memset(identb[:, :], 0.0).then_inc(pool_b, 1)
            nc.gpsimd.memset(identf[:, :], 0.0).then_inc(pool_b, 1)
            nc.gpsimd.memset(causal[:, :], 0.0).then_inc(pool_b, 1)
            pool.wait_ge(pool_b, ONE + 3)
            tri = causal[:, 2 * CH - P:2 * CH]
            nc.gpsimd.affine_select(out=tri, in_=tri, compare_op=ALU.is_ge, fill=LOW, base=0,
                                    pattern=[[-1, P]], channel_multiplier=1).then_inc(const, 1)
            for eye in (identb, identf):
                nc.gpsimd.affine_select(out=eye[:, :], in_=eye[:, :], compare_op=ALU.not_equal, fill=1.0, base=0,
                                        pattern=[[-1, P]], channel_multiplier=1).then_inc(const, 1)

            def body(j):
                for r in range(2):
                    g = 2 * j + r
                    for u, (c, kt) in enumerate(units):
                        if diag[u] is not None:
                            for h in range(HG):
                                n = u * HG + h
                                pool.wait_ge(s_read[n % SB], ONE + PER_BANK[n % SB] * g + n // SB + 1)
                            v = probs[u % 2][:, :, q0s[u]:q0s[u] + P]
                            pool.sem_inc(carrier, 1)
                            nc.gpsimd.affine_select(out=v, in_=v, compare_op=ALU.is_ge, fill=0.0, base=0,
                                                    pattern=[[0, HG], [1, P]], channel_multiplier=-1
                                                    ).then_inc(masked, 1)

            with pool.Fori(0, GROUPS // 2) as j:
                body(j)

        @block.scalar
        def _(act):
            def body(j):
                for r in range(2):
                    g = 2 * j + r

                    def copy_out(n):
                        u, i, use = ends[n], n % 2, 2 * g + n // 2
                        act.wait_ge(pv_ok[u % 2], ONE + PER_SLOT * g + u // 2 + 1)
                        act.wait_ge(oT_ps[i], ONE + use)
                        nc.scalar.copy(ot[i][:, :], psO[:, :]).then_inc(o_copied, 1)

                    for u, (c, kt) in enumerate(units):
                        q0 = q0s[u]
                        act.wait_ge(pv_ok[u % 2], ONE + PER_SLOT * g + u // 2)
                        for h in range(HG):
                            n = u * HG + h
                            act.wait_ge(s_ps, ONE + NU * HG * g + n + 1)
                            nc.scalar.activation(probs[u % 2][:, h, q0:CH], psS[:, n % SB, q0:CH], ACT.Exp,
                                                 scale=SCALE).then_inc(s_read[n % SB], 1)
                        if u - 1 in ends:
                            copy_out(ends.index(u - 1))
                    copy_out(CHUNKS - 1)

            with act.Fori(0, GROUPS // 2) as j:
                body(j)

        @block.vector
        def _(dve):
            MS = 5

            def parts(g, c):
                at = MS * (CHUNKS * g + CHUNKS - 1 - c)
                n = last_of[c]
                for k in (n - 1, n):
                    dve.wait_ge(first_ok[k % 2], ONE + NI // 2 * g + k // 2 + 1)
                nc.vector.tensor_reduce(nm[:, :], blk[:, c * MQ:(c + 1) * MQ, :], AX.X, ALU.max, negate=True
                                        ).then_inc(m_step, 1)
                dve.wait_ge(m_step, ONE + at + 1)
                nc.vector.tensor_copy(nmp[:, 0, :], nm[:, :]).then_inc(m_step, 1)
                dve.wait_ge(m_step, ONE + at + 2)
                nc.vector.tensor_tensor(nm[:, :], nm[:, :], nmp[:, 0, :], ALU.subtract).then_inc(m_step, 1)
                dve.wait_ge(m_step, ONE + at + 3)
                nc.vector.tensor_copy(nmp[:, 1, :], nm[:, :]).then_inc(m_step, 1)
                dve.wait_ge(m_step, ONE + at + 4)
                nc.vector.tensor_tensor(nmp[:, 2, :], nm[:, :], nmp[:, 1, :], ALU.subtract).then_inc(m_step, 1)

            def first(g, n, before):
                slot = n % 2
                dve.wait_ge(first_ps[slot], ONE + NI // 2 * g + n // 2 + 1)
                if items[n][0] == "m":
                    c = items[n][1]
                    sm, count = before(c)
                    if sm is not None:
                        dve.wait_ge(sm, ONE + 16 * count)
                    nc.vector.tensor_copy(nmT[c % 2][:, :], psP[0:MR * MQ, slot, :].bitcast(BF16)[:, 0:P]
                                          ).then_inc(first_ok[slot], 1)
                    return
                h, qt, k0, keys, last = items[n]
                m = blk[:, qt // CT * MQ + h * CT + qt % CT, int(last):int(last) + 1]
                if last:
                    dve.sem_inc(carrier, 1)
                    ins = nc.vector.tensor_tensor_reduce(trash[:, slot, 0:keys], psP[:, slot, 0:keys],
                                                         causal[:, 2 * CH - keys:2 * CH], 1.0, LOW,
                                                         ALU.add, ALU.max, m)
                else:
                    ins = nc.vector.tensor_reduce(m, psP[:, slot, 0:keys], AX.X, ALU.max)
                ins.then_inc(first_ok[slot], 1)
                if n == last_of[qt // CT]:
                    parts(g, qt // CT)

            def normalise(j, r, n):
                g = 2 * j + r
                c, at = CHUNKS - 1 - n, CHUNKS * g + n
                t = psO[:, :].rearrange("p (t h w) -> p t h w", t=CT, h=HG)
                dve.wait_ge(oT_ps[n % 2], ONE + 2 * g + n // 2 + 1)
                nc.vector.reciprocal(rs[:, :, :], t[:, :, :, HD]).then_inc(r_ok, 1)
                dve.wait_ge(r_ok, ONE + at + 1)
                dst = on[:, bass.ds(j, 1), c * CT:(c + 1) * CT, r * GR:(r + 1) * GR].rearrange("p o t (h w) -> p (o t) h w", h=HG)
                nc.vector.tensor_tensor(dst, t[:, :, :, 0:HD],
                                        rs[:, :, :].unsqueeze(3).to_broadcast([P, CT, HG, HD]), ALU.mult
                                        ).then_inc(o_norm, 1)

            nc.vector.memset(blk[:, :, :], LOW).then_inc(const, 1)
            nc.vector.memset(nmp[:, :, :], 0.0).then_inc(const, 1)
            for r in range(2):
                nc.vector.memset(Ks[r][PR:PR + MR, :, :, :], 1.0).then_inc(const, 1)
            dve.wait_ge(const, ONE + 7)
            for n in range(NI):
                first(0, n, lambda c: (m_in[0][c + 2], 1) if c < 2 else (None, 0))

            def body(j, last):
                for r in range(2):
                    g = 2 * j + r

                    def before(c):
                        return (m_in[1 - r][c + 2], j + r + 1) if c < 2 else (m_in[r][c - 2], j + 1)

                    more = not (last and r == 1)
                    for u in range(NU):
                        todo = list(plan[u]) if more else []
                        if todo:
                            first(g + 1, todo.pop(0), before)
                        if u - 2 in ends:
                            normalise(j, r, ends.index(u - 2))
                        for n in todo:
                            first(g + 1, n, before)
                    if more:
                        first(g + 1, NI - 1, before)
                    normalise(j, r, CHUNKS - 1)

            with dve.Fori(0, GROUPS // 2 - 1) as j:
                body(j, False)
            body(GROUPS // 2 - 1, True)

        @block.tensor
        def _(pe):
            def first(g, r, n):
                slot = n % 2
                if items[n][0] == "m":
                    pe.wait_ge(m_step, ONE + 5 * (CHUNKS * g + CHUNKS - items[n][1]))
                    pe.wait_ge(first_ok[slot], ONE + NI // 2 * g + n // 2)
                    pe.transpose(psP[:, slot, :].bitcast(BF16)[:, 0:P], nmp[:, :, :].rearrange("p m n -> p (m n)"),
                                 identb[:, :]).then_inc(first_ps[slot], 1)
                    return
                h, qt, k0, keys, last = items[n]
                pe.wait_ge(first_ok[slot], ONE + NI // 2 * g + n // 2)
                for k in range(0, keys, CH):
                    w = min(CH, keys - k)
                    ins = pe.matmul(psP[:, slot, k:k + w], q_rows(r, h, qt), Ks[r][0:PR, (k0 + k) // CH, h, 0:w],
                                    start=True, stop=True)
                ins.then_inc(first_ps[slot], 1)

            def arrived(j, r):
                for c in range(CHUNKS):
                    pe.wait_ge(kv_in[r][c], ONE + 16 * LOADS * (j + 1))

            pe.wait_ge(const, ONE + 7)
            arrived(0, 0)
            for n in range(NI):
                first(0, 0, n)

            def body(j, last):
                for r in range(2):
                    g = 2 * j + r
                    more = not (last and r == 1)

                    def scores(u, h):
                        n, q0 = u * HG + h, q0s[u]
                        c, kt = units[u]
                        if h == 0 and kt == 0:
                            pe.wait_ge(m_in[r][c], ONE + 16 * (j + 1))
                        pe.wait_ge(s_read[n % SB], ONE + PER_BANK[n % SB] * g + n // SB)
                        pe.matmul(psS[:, n % SB, q0:CH], Ks[r][:, kt // CT, h, kt % CT * P:(kt % CT + 1) * P],
                                  Qs[r][:, c, h, q0:CH], start=True, stop=True).then_inc(s_ps, 1)

                    def pv(u):
                        c, kt = units[u]
                        q0, end = q0s[u], u in ends
                        if diag[u] is None:
                            for h in range(HG):
                                n = u * HG + h
                                pe.wait_ge(s_read[n % SB], ONE + PER_BANK[n % SB] * g + n // SB + 1)
                        else:
                            pe.wait_ge(masked, ONE + DG * g + sum(d is not None for d in diag[:u]) + 1)
                        if kt == 0:
                            pe.wait_ge(o_norm, ONE + CHUNKS * g + (CHUNKS - 1 - c))
                        for h in range(HG):
                            ins = pe.matmul(psO[h * VW:(h + 1) * VW, q0:CH], Vs[r][:, kt, h * VW:(h + 1) * VW],
                                            probs[u % 2][:, h, q0:CH], start=(kt == 0), stop=end,
                                            tile_position=(0, h * VW))
                        ins.then_inc(pv_ok[u % 2], 1)

                    def turn(n):
                        pe.wait_ge(o_copied, ONE + CHUNKS * g + n + 1)
                        for t in range(CT):
                            ins = pe.transpose(psO[:, t * P:(t + 1) * P], ot[n % 2][:, t * P:(t + 1) * P],
                                               identf[:, :])
                        ins.then_inc(oT_ps[n % 2], 1)

                    for u in range(NU):
                        todo = list(plan[u]) if more else []
                        if u == START and more:
                            arrived(j + r, 1 - r)
                        scores(u, 0)
                        scores(u, 1)
                        if todo:
                            first(g + 1, 1 - r, todo.pop(0))
                        if u - 2 in ends:
                            turn(ends.index(u - 2))
                        scores(u, 2)
                        if todo:
                            first(g + 1, 1 - r, todo.pop(0))
                        scores(u, 3)
                        if u > 0:
                            pv(u - 1)
                        while todo:
                            first(g + 1, 1 - r, todo.pop(0))
                    if more:
                        first(g + 1, 1 - r, NI - 1)
                    pv(NU - 1)
                    turn(CHUNKS - 1)

            with pe.Fori(0, GROUPS // 2 - 1) as j:
                body(j, False)
            body(GROUPS // 2 - 1, True)


def output(nc, wout, acc, on, out):
    with ExitStack() as ctx:
        sem = lambda n: ctx.enter_context(nc.semaphore(n))
        wo = ctx.enter_context(nc.sbuf_tensor("wo", [P, KC, D], F32))
        ident = ctx.enter_context(nc.sbuf_tensor("ident_c", [P, P], F32))
        aT = [ctx.enter_context(nc.sbuf_tensor(f"aT{i}", [P, KC, P], F32)) for i in range(2)]
        psT = ctx.enter_context(nc.psum_tensor("psT_c", [P, 4, CH], F32))
        ps = ctx.enter_context(nc.psum_tensor("ps", [P, 4, CH], F32))
        w_in = sem("wo_in")
        eye = sem("eye")
        t_ps = sem("t_ps")
        t_ok = sem("t_ok")
        o_ps = sem("o_ps")
        o_add = sem("o_add")
        o_out = sem("o_out")
        block = ctx.enter_context(nc.Block())

        @block.sync
        def _(sp):
            sp.dma_start(wo[:, :, :], wout.rearrange("(k p) n -> p k n", p=P)).then_inc(w_in, 16)
            for c in range(TILES // CT):
                sp.wait_ge(o_add, CT * (c + 1))
                sp.dma_start(out[c // CHUNKS, c % CHUNKS * CH:(c % CHUNKS + 1) * CH, :]
                             .rearrange("(t p) d -> p t d", p=P), acc[:, c * CT:(c + 1) * CT, :]).then_inc(o_out, 16)
            sp.wait_ge(o_out, 16 * TILES // CT)

        @block.gpsimd
        def _(pool):
            nc.gpsimd.memset(ident[:, :], 0.0).then_inc(eye, 1)
            pool.wait_ge(eye, 1)
            nc.gpsimd.affine_select(out=ident[:, :], in_=ident[:, :], compare_op=ALU.not_equal, fill=1.0, base=0,
                                    pattern=[[-1, P]], channel_multiplier=1).then_inc(eye, 1)

        @block.tensor
        def _(pe):
            def turn(t):
                if t >= 4:
                    pe.wait_ge(t_ok, t - 3)
                for k in range(KC):
                    ins = pe.transpose(psT[:, t % 4, k * P:(k + 1) * P], on[:, t // TT * KC + k, t % TT, :], ident[:, :])
                ins.then_inc(t_ps, 1)

            pe.wait_ge(eye, 2)
            pe.wait_ge(w_in, 16)
            turn(0)
            for t in range(TILES):
                if t + 1 < TILES:
                    turn(t + 1)
                pe.wait_ge(t_ok, t + 1)
                if t >= 4:
                    pe.wait_ge(o_add, t - 3)
                for k in range(KC):
                    ins = pe.matmul(ps[:, t % 4, 0:D], aT[t % 2][:, k, :], wo[:, k, :],
                                    start=(k == 0), stop=(k == KC - 1))
                ins.then_inc(o_ps, 1)

        @block.scalar
        def _(act):
            for t in range(TILES):
                act.wait_ge(t_ps, t + 1)
                if t >= 2:
                    act.wait_ge(o_ps, t - 1)
                nc.scalar.copy(aT[t % 2][:, :, :].rearrange("p k n -> p (k n)"), psT[:, t % 4, 0:D]).then_inc(t_ok, 1)

        @block.vector
        def _(dve):
            for t in range(TILES):
                dve.wait_ge(o_ps, t + 1)
                nc.vector.tensor_tensor(acc[:, t, :], ps[:, t % 4, 0:D], acc[:, t, :], ALU.add).then_inc(o_add, 1)


def build(nc, x, wqk, wvg, wout, bout, gb, we, be, cos, sin, out):
    qk_s = nc.dram_tensor("qk_scratch", [2, GROUPS, 3, HD, CHUNKS, HG, CH], BF16, kind="Internal").ap()
    v_s = nc.dram_tensor("v_scratch", [GROUPS, P, TT, HG * VW], F32, kind="Internal").ap()
    with nc.sbuf_tensor("acc", [P, TILES, D], F32) as acc:
        project(nc, x, wqk, wvg, we, be, bout, gb, cos, sin, qk_s, v_s, acc)
        with nc.sbuf_tensor("on", [P, B * KC, TT, P], F32) as on:
            attend(nc, qk_s, v_s, on)
            output(nc, wout, acc, on, out)


def rotary_tables():
    inv = (1.0 / np.float32(10000.0) ** (np.arange(0, HD, 2, dtype=np.float32) / np.float32(HD))).astype(np.float32)
    f = np.arange(N, dtype=np.float32)[None, :] * np.tile(np.repeat(inv, 2), P // HD)[:, None]
    sign = np.where(np.arange(P) % 2 == 0, -1.0, 1.0).astype(np.float32)[:, None]
    return np.cos(f).astype(np.float32), (np.sin(f) * sign).astype(np.float32)


def kernel(L0_attn_X, L0_attn_Wqkv, L0_attn_Wout, L0_attn_bout, L0_ffn_gate_w, L0_ffn_gate_b, L0_ffn_expert_w,
           L0_ffn_expert_b):
    import concourse.bacc as bacc
    from concourse.bass_utils import run_bass_kernel_spmd

    wqkv = np.asarray(L0_attn_Wqkv)
    cos, sin = rotary_tables()
    arrays = {
        "x": np.ascontiguousarray(L0_attn_X),
        "wqk": np.ascontiguousarray(wqkv[:, :2 * D]),
        "wvg": np.ascontiguousarray(np.concatenate([wqkv[:, 2 * D:], np.asarray(L0_ffn_gate_w).T], axis=1)),
        "wout": np.ascontiguousarray(L0_attn_Wout),
        "bout": np.asarray(L0_attn_bout).reshape(1, D),
        "gb": np.asarray(L0_ffn_gate_b).reshape(1, GATES),
        "we": np.ascontiguousarray(L0_ffn_expert_w),
        "be": np.ascontiguousarray(L0_ffn_expert_b),
        "cos": cos,
        "sin": sin,
    }
    nc = bacc.Bacc("TRN2", target_bir_lowering=False, num_devices=1)
    args = [nc.dram_tensor(n, a.shape, mybir.dt.from_np(a.dtype), kind="ExternalInput").ap()
            for n, a in arrays.items()]
    out = nc.dram_tensor("out", (B, N, D), F32, kind="ExternalOutput").ap()
    build(nc, *args, out)
    r = run_bass_kernel_spmd(nc, [arrays], core_ids=[0])
    return r.results[0]["out"]
```

```python
from contextlib import ExitStack

import numpy as np

import concourse.bass as bass
from concourse import mybir

ALU = mybir.AluOpType
ACT = mybir.ActivationFunctionType
AX = mybir.AxisListType
F32 = mybir.dt.float32
BF16 = mybir.dt.bfloat16
U32 = mybir.dt.uint32
F16 = mybir.dt.float16

P = 128
B, N, D = 2, 2048, 256
HEADS, HD = 16, 16
EXPERTS, GATES = 8, 10
EPS = 1e-5
SCALE = HD ** -0.5
KC = D // P
TT = N // P
TILES = B * TT
CH = 512
CT = CH // P
CHUNKS = N // CH
QKT = 2 * D // P
HG = 4
GROUPS = B * HEADS // HG
GR = HG * HD
VW = 32
BLOCKS = ((3, 0), (2, 1), (1, 2))
PR = sum(n for n, _ in BLOCKS) * HD
MR = 3
LOW = -3.0e38
XSCALE = 2.0 ** 11
ONE = 1


def project(nc, x, wqk, wvg, we, be, bout, gb, cos, sin, qk_s, v_s, acc):
    with ExitStack() as ctx:
        sb = lambda n, s, d=F32: ctx.enter_context(nc.sbuf_tensor(n, s, d))
        sems = []

        def sem(n):
            sems.append(ctx.enter_context(nc.semaphore(n)))
            return sems[-1]

        pair = lambda n: [sem(f"{n}{i}") for i in range(2)]

        ident = sb("ident", [P, P])
        wqk_sb = sb("wqk_sb", [P, KC, 2 * D])
        wvg_sb = sb("wvg_sb", [P, KC, D + GATES])
        we_sb = sb("we_sb", [P, KC, EXPERTS * D])
        be_sb = sb("be_sb", [EXPERTS + 1, D])
        gb_sb = sb("gb_sb", [P, GATES])
        trig = sb("trig", [P, 2, CH])
        iota = sb("iota", [P, GATES])
        eps = sb("eps", [P, 1])
        xn = [sb(f"xn{i}", [P, CT, D]) for i in range(2)]
        xnT = [sb(f"xnT{i}", [P, KC, CH]) for i in range(2)]
        xp = [sb(f"xp{i}", [P, 2, KC, CH], F16) for i in range(2)]
        wp = sb("wp", [P, 2, KC, EXPERTS * D], F16)
        wqp = sb("wqp", [P, 2, KC, 2 * D], F16)
        wvp = sb("wvp", [P, 2, KC, D + GATES], F16)
        OF_E, OF_QK, OF_V, OF_G = range(4)
        whalf = sb("whalf", [P, 2 * KC])
        wmax = sb("wmax", [P, 4])
        wrow = sb("wrow", [P, 4, P])
        wexp = sb("wexp", [P, 4])
        wscale = sb("wscale", [P, 4])
        unscale = sb("unscale", [P, 4])
        qs = [sb(f"qs{i}", [P, CH]) for i in range(2)]
        stat = sb("stat", [P, CT, 6])
        mv = sb("mv", [P, CT, 2])
        std = sb("std", [P, CT])
        rstd = sb("rstd", [P, CT])
        vst = [sb(f"vst{i}", [P, CT, HEADS, VW]) for i in range(2)]
        lg = [sb(f"lg{i}", [P, CT, GATES]) for i in range(2)]
        gl = sb("gl", [P, CT, GATES])
        ge = sb("ge", [P, CT, GATES])
        gp = sb("gp", [P, CT, GATES])
        gm = sb("gm", [P, CT])
        gr = sb("gr", [P, CT])
        top = sb("top", [P, CT, 8])
        topi = sb("topi", [P, CT, 8], U32)
        topf = sb("topf", [P, CT, 2])
        hot = sb("hot", [P, 2, CT, GATES])
        cw = sb("cw", [P, CT, EXPERTS])
        den = sb("den", [P, CT])
        dez = sb("dez", [P, CT])
        c9 = [sb(f"c9{i}", [P, CT, EXPERTS + 1]) for i in range(2)]
        cs = [sb(f"cs{i}", [P, CT, EXPERTS]) for i in range(2)]
        c9T = sb("c9T", [EXPERTS + 1, CH])
        odd = [sb(f"odd{i}", [P, D]) for i in range(2)]
        rot = [sb(f"rot{i}", [P, CH]) for i in range(QKT)]
        swp = [sb(f"swp{i}", [P, CH]) for i in range(QKT)]
        part = [sb(f"part{i}", [P, 3, CH], BF16) for i in range(QKT)]

        psT = ctx.enter_context(nc.psum_tensor("psT", [P, 2, CH], F32))
        psQ = ctx.enter_context(nc.psum_tensor("psQ", [P, CH], F32))
        psM = ctx.enter_context(nc.psum_tensor("psM", [P, 4, CH], F32))
        psB = ctx.enter_context(nc.psum_tensor("psB", [P, D], F32))

        x_in = [ctx.enter_context(nc.semaphore(f"x_in{i}")) for i in range(3)]
        w2_in = [ctx.enter_context(nc.semaphore(f"w2_in{i}")) for i in range(2)]
        w_in = sem("w_in")
        trig_in = sem("trig_in")
        const = sem("const")
        vcol = sem("vcol")
        stats = sem("stats")
        std_ok = sem("std_ok")
        xn_ok = sem("xn_ok")
        xT_ps = sem("xT_ps")
        xT_ok = sem("xT_ok")
        xh_ok = sem("xh_ok")
        xl_ok = sem("xl_ok")
        wm_ok = sem("wm_ok")
        wm_ps = sem("wm_ps")
        wh_ok = sem("wh_ok")
        wl_ok = sem("wl_ok")
        w_step = sem("w_step")
        vg_ps = sem("vg_ps")
        vg_ok = sem("vg_ok")
        v_stored = pair("v_stored")
        gate_in = sem("gate_in")
        gate_e = sem("gate_e")
        gate_c = sem("gate_c")
        qk_ps = sem("qk_ps")
        qk_ok = sem("qk_ok")
        each = lambda n: [sem(f"{n}{k}") for k in range(QKT)]
        rope_ok = each("rope_ok")
        sum_ok = each("sum_ok")
        high_ok = each("high_ok")
        rest_ok = each("rest_ok")
        mid_ok = each("mid_ok")
        split_ok = each("split_ok")
        part_stored = each("part_stored")
        moe_ps = sem("moe_ps")
        moe_read = [sem(f"moe_read{i}") for i in range(4)]
        cT_ps = sem("cT_ps")
        cT_ok = sem("cT_ok")
        bias_ps = sem("bias_ps")
        bias_read = sem("bias_read")
        acc_ok = sem("acc_ok")
        carrier = sem("carrier")
        norm_step = sem("norm_step")
        gate_step = sem("gate_step")
        sum_step = sem("sum_step")
        pool_step = sem("pool_step")

        STORES = 3 * P // GR
        WS = 5
        QKV_PARTS = ((wqp, wqk_sb, slice(0, 2 * D), OF_QK), (wvp, wvg_sb, slice(0, D), OF_V),
                     (wvp, wvg_sb, slice(D, D + GATES), OF_G))
        NB = B
        block = ctx.enter_context(nc.Block())

        @block.sync
        def _(sp):
            def load_x(s, into):
                j, b = divmod(s, NB)
                sp.dma_start(acc[:, b * TT + j * CT:b * TT + (j + 1) * CT, :],
                             x[b, j * CH:(j + 1) * CH, :].rearrange("(t p) d -> p t d", p=P)).then_inc(into, 16)

            def load_trig(j):
                sp.dma_start(trig[:, 0, :], cos[:, bass.ds(j * CH, CH)]).then_inc(trig_in, 16)
                sp.dma_start(trig[:, 1, :], sin[:, bass.ds(j * CH, CH)]).then_inc(trig_in, 16)

            load_x(0, x_in[0])
            sp.dma_start(wvg_sb[:, :, :], wvg.rearrange("(k p) n -> p k n", p=P)).then_inc(w_in, 16)
            sp.dma_start(wqk_sb[:, :, :], wqk.rearrange("(k p) n -> p k n", p=P)).then_inc(w_in, 16)
            sp.dma_start(gb_sb[:, :], gb.partition_broadcast(P)).then_inc(w_in, 16)
            load_trig(0)
            load_x(1, x_in[1])
            for e in range(EXPERTS):
                sp.dma_start(we_sb[:, :, e * D:(e + 1) * D],
                             we[e].rearrange("(k p) n -> p k n", p=P)).then_inc(w2_in[2 * e // EXPERTS], 16)
            sp.dma_start(be_sb[0:EXPERTS, :], be).then_inc(w2_in[1], 16)
            sp.dma_start(be_sb[EXPERTS:EXPERTS + 1, :], bout).then_inc(w2_in[1], 16)
            for s in range(2, NB * CHUNKS):
                load_x(s, x_in[2])

            def stores(s, j, b, before_last):
                sp.wait_ge(vg_ok, ONE + s * CT + CT)
                for h in range(HEADS // HG):
                    sp.dma_start(v_s[b * (HEADS // HG) + h, :, bass.ds(j * CT, CT), :],
                                 vst[b][:, :, h * HG:(h + 1) * HG, :].rearrange("p t h w -> p t (h w)")
                                 ).then_inc(v_stored[b], 16)
                for k in range(QKT):
                    if k == 1 and b == 1 and before_last:
                        for q in range(QKT):
                            sp.wait_ge(rope_ok[q], ONE + s + 1)
                            sp.wait_ge(sum_ok[q], ONE + s + 1)
                        sp.sem_inc(carrier, 1)
                        load_trig(j + 1)
                    sp.wait_ge(split_ok[k], ONE + s + 1)
                    for i in range(P // GR):
                        for p in range(3):
                            dst = qk_s[k // 2, b * (HEADS // HG) + k % 2 * (P // GR) + i, p, :, bass.ds(j, 1), :, :]
                            sp.dma_start(dst.rearrange("d o h n -> h d (o n)"),
                                         part[k][i * GR:(i + 1) * GR, p, :]).then_inc(part_stored[k], 16)

            with sp.Fori(0, CHUNKS - 1) as j:
                for b in range(NB):
                    stores(2 * j + b, j, b, True)
            for b in range(NB):
                stores(2 * (CHUNKS - 1) + b, CHUNKS - 1, b, False)
            for b in range(2):
                sp.wait_ge(v_stored[b], ONE + 16 * (HEADS // HG) * CHUNKS)
            for k in range(QKT):
                sp.wait_ge(part_stored[k], ONE + 16 * STORES * NB * CHUNKS)

        @block.gpsimd
        def _(pool):
            for every in sems:
                pool.sem_inc(every, ONE)
            steps = [0]

            def step(ins):
                steps[0] += 1
                return ins.then_inc(pool_step, 1)

            nc.gpsimd.memset(eps[:, :], EPS).then_inc(const, 1)
            step(nc.gpsimd.memset(ident[:, :], 0.0))
            pool.wait_ge(pool_step, ONE + 1)
            nc.gpsimd.affine_select(out=ident[:, :], in_=ident[:, :], compare_op=ALU.not_equal, fill=1.0, base=0,
                                    pattern=[[-1, P]], channel_multiplier=1).then_inc(const, 1)
            nc.gpsimd.iota(iota[:, :], pattern=[[1, GATES]], base=0, channel_multiplier=0,
                           allow_small_or_imprecise_dtypes=True).then_inc(const, 1)
            for b in range(NB):
                nc.gpsimd.memset(vst[b][:, :, :, :], 1.0).then_inc(const, 1)
                nc.gpsimd.memset(c9[b][:, :, :], 1.0).then_inc(const, 1)

            def body(j):
                pool.wait_ge(trig_in, ONE + 32 * j + 32)
                for b in range(NB):
                    s = 2 * j + b

                    def rotate(k):
                        pool.wait_ge(rope_ok[k], ONE + s + 1)
                        step(nc.gpsimd.tensor_tensor(swp[k][:, :], swp[k][:, :], trig[:, 1, :], ALU.mult))
                        pool.wait_ge(pool_step, ONE + 1 + QKT * s + k + 1)
                        nc.gpsimd.tensor_tensor(rot[k][:, :], rot[k][:, :], swp[k][:, :], ALU.add
                                                ).then_inc(sum_ok[k], 1)

                    def rest(k):
                        pool.wait_ge(high_ok[k], ONE + s + 1)
                        nc.gpsimd.tensor_tensor(rot[k][:, :], rot[k][:, :], part[k][:, 0, :], ALU.subtract
                                                ).then_inc(rest_ok[k], 1)

                    def third(k):
                        pool.wait_ge(mid_ok[k], ONE + s + 1)
                        nc.gpsimd.tensor_tensor(part[k][:, 2, :], rot[k][:, :], part[k][:, 1, :], ALU.subtract
                                                ).then_inc(split_ok[k], 1)

                    rotate(0)
                    rotate(1)
                    rest(0)
                    rotate(2)
                    rest(1)
                    third(0)
                    rotate(3)
                    rest(2)
                    third(1)
                    rest(3)
                    third(2)
                    third(3)

            with pool.Fori(0, CHUNKS) as j:
                body(j)

        @block.scalar
        def _(act):
            def deviation(s):
                act.wait_ge(stats, ONE + s + 1)
                nc.scalar.activation(std[:, :], mv[:, :, 1], ACT.Sqrt, bias=eps[:, :]).then_inc(std_ok, 1)

            def copy_xT(s, b):
                for k in range(KC):
                    act.wait_ge(xT_ps, ONE + KC * s + k + 1)
                    nc.scalar.copy(xnT[b][:, k, :], psT[:, k, :]).then_inc(xT_ok, 1)
                    nc.scalar.activation(xp[b][:, 0, k, :], psT[:, k, :], ACT.Copy, scale=XSCALE).then_inc(xh_ok, 1)

            def unscaled(out, ps, of, first):
                if first:
                    return nc.scalar.copy(out, ps)
                return nc.scalar.activation(out, ps, ACT.Copy, scale=unscale[:, of:of + 1])

            def copy_v(s, j, b, first=False):
                act.wait_ge(v_stored[b], ONE + 16 * (HEADS // HG) * j)
                for t in range(CT):
                    act.wait_ge(vg_ps, ONE + CT * s + t + 1)
                    unscaled(vst[b][:, t, :, 0:HD], psT[:, t % 2, 0:D].rearrange("p (h d) -> p h d", d=HD), OF_V,
                             first).then_inc(vcol, 1)
                    unscaled(lg[b][:, t, :], psT[:, t % 2, D:D + GATES], OF_G, first).then_inc(vg_ok, 1)
                act.wait_ge(gate_in, ONE + s + 1)
                nc.scalar.activation(ge[:, :, :], gl[:, :, :], ACT.Exp).then_inc(gate_e, 1)

            def copy_q(s, k, first=False):
                act.wait_ge(qk_ps, ONE + QKT * s + k + 1)
                act.wait_ge(rope_ok[(k - 2) % QKT], ONE + s + k // 2)
                unscaled(qs[k % 2][:, :], psQ[:, :], OF_QK, first).then_inc(qk_ok, 1)

            def high(s, k):
                act.wait_ge(sum_ok[k], ONE + s + 1)
                act.wait_ge(part_stored[k], ONE + 16 * STORES * s)
                nc.scalar.copy(part[k][:, 0, :], rot[k][:, :]).then_inc(high_ok[k], 1)

            def mid(s, k):
                act.wait_ge(rest_ok[k], ONE + s + 1)
                nc.scalar.copy(part[k][:, 1, :], rot[k][:, :]).then_inc(mid_ok[k], 1)

            def high_w(parts, whole, cols, of):
                nc.scalar.activation(parts[:, 0, :, cols], whole[:, :, cols], ACT.Copy, scale=wscale[:, of:of + 1]
                                     ).then_inc(wh_ok, 1)

            act.wait_ge(const, ONE + 1)
            deviation(0)
            copy_xT(0, 0)
            deviation(1)
            act.wait_ge(const, ONE + 7)
            copy_v(0, 0, 0, True)
            copy_q(0, 0, True)
            copy_q(0, 1, True)
            act.wait_ge(w_step, ONE + WS + 4)
            for e in range(EXPERTS):
                if e == EXPERTS // 2:
                    copy_q(0, 2, True)
                high_w(wp, we_sb, slice(e * D, (e + 1) * D), OF_E)
            copy_q(0, 3, True)
            for parts, whole, cols, of in QKV_PARTS:
                high_w(parts, whole, cols, of)
            high(0, 0)
            for k in range(1, QKT):
                high(0, k)
                mid(0, k - 1)
            mid(0, QKT - 1)

            def body(j, last):
                for b in range(NB):
                    s = 2 * j + b
                    if last and b == 1:
                        continue
                    copy_xT(s + 1, 1 - b)
                    if not last:
                        deviation(s + 2)
                    copy_v(s + 1, j + b, 1 - b)
                    copy_q(s + 1, 0)
                    copy_q(s + 1, 1)
                    high(s + 1, 0)
                    copy_q(s + 1, 2)
                    copy_q(s + 1, 3)
                    high(s + 1, 1)
                    mid(s + 1, 0)
                    high(s + 1, 2)
                    mid(s + 1, 1)
                    high(s + 1, 3)
                    mid(s + 1, 2)
                    mid(s + 1, 3)

            with act.Fori(0, CHUNKS - 1) as j:
                body(j, False)
            body(CHUNKS - 1, True)

        @block.vector
        def _(dve):
            def tile_of(j, b, t):
                return acc[:, bass.ds(j * CT + b * TT + t, 1), :].rearrange("p o d -> p (o d)")

            def norm_a(s, j, b):
                base = (CT + 1) * s
                for t in range(CT):
                    dve.sem_inc(carrier, 1)
                    nc.vector.bn_stats(stat[:, t, :], tile_of(j, b, t)).then_inc(norm_step, 1)
                for t in range(CT):
                    dve.wait_ge(norm_step, ONE + base + t + 1)
                    dve.sem_inc(carrier, 1)
                    ins = nc.vector.bn_aggr(mv[:, t, :], stat[:, t, :])
                ins.then_inc(stats, 1)

            def norm_c(s, j, b):
                dve.wait_ge(std_ok, ONE + s + 1)
                nc.vector.reciprocal(rstd[:, :], std[:, :]).then_inc(norm_step, 1)
                dve.wait_ge(norm_step, ONE + (CT + 1) * (s + 1))
                for t in range(CT):
                    ins = nc.vector.tensor_scalar(xn[b][:, t, :], tile_of(j, b, t), mv[:, t, 0:1], rstd[:, t:t + 1],
                                                  ALU.subtract, ALU.mult)
                ins.then_inc(xn_ok, 1)

            def low_x(s, b):
                for k in range(KC):
                    dve.wait_ge(xT_ok, ONE + KC * s + k + 1)
                    dve.wait_ge(xh_ok, ONE + KC * s + k + 1)
                    nc.vector.scalar_tensor_tensor(out=xp[b][:, 1, k, :], in0=xnT[b][:, k, :], scalar=XSCALE,
                                                   in1=xp[b][:, 0, k, :], op0=ALU.mult, op1=ALU.subtract
                                                   ).then_inc(xl_ok, 1)

            def max_qkv():
                for whole, cols, of in ((wqk_sb, slice(0, 2 * D), OF_QK), (wvg_sb, slice(0, D), OF_V),
                                        (wvg_sb, slice(D, D + GATES), OF_G)):
                    ins = nc.vector.tensor_reduce(wmax[:, of:of + 1], whole[:, :, cols], AX.XY, ALU.max,
                                                  apply_absolute_value=True)
                ins.then_inc(w_step, 1)

            def max_w(i):
                dve.wait_ge(w2_in[i], 16 * (EXPERTS // 2 + 2 * i))
                half = we_sb[:, :, i * EXPERTS * D // 2:(i + 1) * EXPERTS * D // 2]
                nc.vector.tensor_reduce(whalf[:, i * KC:(i + 1) * KC], half, AX.X, ALU.max, apply_absolute_value=True
                                        ).then_inc(w_step, 1)

            def max_all():
                dve.wait_ge(w_step, ONE + 3)
                nc.vector.tensor_reduce(wmax[:, OF_E:OF_E + 1], whalf[:, :], AX.X, ALU.max).then_inc(w_step, 1)
                dve.wait_ge(w_step, ONE + 4)
                nc.vector.tensor_copy(wrow[:, :, :], wmax[:, :].unsqueeze(2).to_broadcast([P, 4, P])
                                      ).then_inc(wm_ok, 1)

            def scale_w():
                dve.wait_ge(wm_ps, ONE + 1)
                nc.vector.tensor_reduce(wexp[:, :], psM[:, :, 0:P], AX.X, ALU.max).then_inc(w_step, 1)
                dve.wait_ge(w_step, ONE + WS)
                nc.vector.tensor_scalar_max(wexp[:, :], wexp[:, :], 1e-28).then_inc(w_step, 1)
                dve.wait_ge(w_step, ONE + WS + 1)
                nc.vector.tensor_single_scalar(wexp[:, :].bitcast(U32), wexp[:, :].bitcast(U32), 0x7F800000,
                                               ALU.bitwise_and).then_inc(w_step, 1)
                dve.wait_ge(w_step, ONE + WS + 2)
                nc.vector.tensor_scalar_mul(unscale[:, :], wexp[:, :], 2.0 ** -14 / XSCALE).then_inc(w_step, 1)
                nc.vector.tensor_scalar(wscale[:, :].bitcast(U32), wexp[:, :].bitcast(U32), -1.0,
                                        float((2 * 127 + 14) << 23), ALU.mult, ALU.add).then_inc(w_step, 1)

            def low_w(n, parts, whole, cols, of):
                dve.wait_ge(w_step, ONE + WS + 4)
                dve.wait_ge(wh_ok, ONE + n + 1)
                nc.vector.scalar_tensor_tensor(out=parts[:, 1, :, cols], in0=whole[:, :, cols],
                                               scalar=wscale[:, of:of + 1], in1=parts[:, 0, :, cols],
                                               op0=ALU.mult, op1=ALU.subtract).then_inc(wl_ok, 1)

            def low_e(experts):
                for e in experts:
                    low_w(e, wp, we_sb, slice(e * D, (e + 1) * D), OF_E)

            SWAP = [i ^ 1 for i in range(32)]

            def rope(s, k):
                dve.wait_ge(qk_ok, ONE + QKT * s + k + 1)
                dve.wait_ge(split_ok[k], ONE + s)
                dve.sem_inc(carrier, 1)
                nc.vector.stream_shuffle(swp[k][:, :], qs[k % 2][:, :], SWAP)
                nc.vector.tensor_tensor(rot[k][:, :], qs[k % 2][:, :], trig[:, 0, :], ALU.mult
                                        ).then_inc(rope_ok[k], 1)

            def wide(a):
                return a.unsqueeze(2).to_broadcast([P, CT, GATES])

            def step(ins):
                return ins.then_inc(gate_step, 1)

            GA, GB = 2, 21

            def gates_a(s, b):
                base = (GA + GB) * s
                dve.wait_ge(vg_ok, ONE + CT * s + CT)
                step(nc.vector.tensor_tensor(gl[:, :, :], lg[b][:, :, :],
                                             gb_sb[:, :].unsqueeze(1).to_broadcast([P, CT, GATES]), ALU.add))
                dve.wait_ge(gate_step, ONE + base + 1)
                step(nc.vector.tensor_reduce(gm[:, :], gl[:, :, :], AX.X, ALU.max))
                dve.wait_ge(gate_step, ONE + base + 2)
                nc.vector.tensor_tensor(gl[:, :, :], gl[:, :, :], wide(gm[:, :]), ALU.subtract).then_inc(gate_in, 1)

            def gates_b(s, b):
                base = (GA + GB) * s + GA
                dve.wait_ge(gate_e, ONE + s + 1)
                step(nc.vector.tensor_reduce(gr[:, :], ge[:, :, :], AX.X, ALU.add))
                dve.wait_ge(gate_step, ONE + base + 1)
                step(nc.vector.reciprocal(gr[:, :], gr[:, :]))
                dve.wait_ge(gate_step, ONE + base + 2)
                step(nc.vector.tensor_tensor(gp[:, :, :], ge[:, :, :], wide(gr[:, :]), ALU.mult))
                dve.wait_ge(gate_step, ONE + base + 3)
                for t in range(CT):
                    dve.sem_inc(carrier, 1)
                    step(nc.vector.max(top[:, t, :], gp[:, t, :]))
                for t in range(CT):
                    dve.wait_ge(gate_step, ONE + base + 4 + t)
                    dve.sem_inc(carrier, 1)
                    step(nc.vector.max_index(topi[:, t, :], top[:, t, :], gp[:, t, :]))
                dve.wait_ge(gate_step, ONE + base + 11)
                step(nc.vector.tensor_copy(topf[:, :, :], topi[:, :, 0:2]))
                dve.wait_ge(gate_step, ONE + base + 12)
                for i in range(2):
                    step(nc.vector.tensor_tensor(hot[:, i, :, :], iota[:, :].unsqueeze(1).to_broadcast([P, CT, GATES]),
                                                 topf[:, :, i:i + 1].to_broadcast([P, CT, GATES]), ALU.is_equal))
                dve.wait_ge(gate_step, ONE + base + 14)
                step(nc.vector.tensor_tensor(hot[:, 0, :, :], hot[:, 0, :, :], hot[:, 1, :, :], ALU.add))
                dve.wait_ge(gate_step, ONE + base + 15)
                step(nc.vector.tensor_tensor(cw[:, :, :], gp[:, :, 0:EXPERTS], hot[:, 0, :, 0:EXPERTS], ALU.mult))
                dve.wait_ge(gate_step, ONE + base + 16)
                step(nc.vector.tensor_reduce(den[:, :], cw[:, :, :], AX.X, ALU.add))
                dve.wait_ge(gate_step, ONE + base + 17)
                step(nc.vector.tensor_single_scalar(dez[:, :], den[:, :], 0.0, ALU.is_le))
                dve.wait_ge(gate_step, ONE + base + 18)
                step(nc.vector.tensor_tensor(den[:, :], den[:, :], dez[:, :], ALU.add))
                dve.wait_ge(gate_step, ONE + base + 19)
                step(nc.vector.reciprocal(den[:, :], den[:, :]))
                dve.wait_ge(gate_step, ONE + base + 20)
                step(nc.vector.tensor_tensor(c9[b][:, :, 0:EXPERTS], cw[:, :, :],
                                             den[:, :].unsqueeze(2).to_broadcast([P, CT, EXPERTS]), ALU.mult))
                dve.wait_ge(gate_step, ONE + base + 21)
                nc.vector.tensor_scalar(cs[b][:, :, :], c9[b][:, :, 0:EXPERTS], unscale[:, OF_E:OF_E + 1], None, ALU.mult
                                        ).then_inc(gate_c, 1)

            def combine(s, j, b, t, banks):
                use = CT * s + t
                base = (EXPERTS // 2) * use
                rows = tile_of(j, b, t)
                dve.wait_ge(gate_c, ONE + s + 1)
                for n in banks:
                    dve.wait_ge(moe_ps, ONE + base + n + 1)
                    e = 2 * n
                    if n > 0:
                        dve.wait_ge(sum_step, ONE + base + n)
                    nc.vector.scalar_tensor_tensor(out=rows, in0=psM[:, n, 0:D], scalar=cs[b][:, t, e:e + 1],
                                                   in1=rows, op0=ALU.mult, op1=ALU.add).then_inc(sum_step, 1)
                    if n == 0:
                        ins = nc.vector.tensor_scalar(odd[t % 2][:, :], psM[:, n, D:2 * D],
                                                      cs[b][:, t, e + 1:e + 2], None, ALU.mult)
                    else:
                        dve.wait_ge(moe_read[n - 1], ONE + use + 1)
                        ins = nc.vector.scalar_tensor_tensor(out=odd[t % 2][:, :], in0=psM[:, n, D:2 * D],
                                                             scalar=cs[b][:, t, e + 1:e + 2], in1=odd[t % 2][:, :],
                                                             op0=ALU.mult, op1=ALU.add)
                    ins.then_inc(moe_read[n], 1)
                if EXPERTS // 2 - 1 in banks:
                    dve.wait_ge(bias_ps, ONE + use + 1)
                    dve.wait_ge(moe_read[EXPERTS // 2 - 1], ONE + use + 1)
                    nc.vector.tensor_tensor(odd[t % 2][:, :], psB[:, :], odd[t % 2][:, :], ALU.add
                                            ).then_inc(bias_read, 1)
                    dve.wait_ge(sum_step, ONE + base + EXPERTS // 2)
                    dve.wait_ge(bias_read, ONE + use + 1)
                    nc.vector.tensor_tensor(rows, rows, odd[t % 2][:, :], ALU.add).then_inc(acc_ok, 1)

            ALL = range(EXPERTS // 2)
            HALVES = (ALL[:2], ALL[2:])
            dve.wait_ge(const, ONE + 1)
            dve.wait_ge(x_in[0], 16)
            norm_a(0, 0, 0)
            norm_c(0, 0, 0)
            dve.wait_ge(w_in, ONE + 48)
            max_qkv()
            dve.wait_ge(x_in[1], 16)
            norm_a(1, 0, 1)
            norm_c(1, 0, 1)
            dve.wait_ge(trig_in, ONE + 32)
            low_x(0, 0)
            max_w(0)
            max_w(1)
            max_all()
            dve.wait_ge(const, ONE + 7)
            gates_a(0, 0)
            scale_w()
            rope(0, 0)
            rope(0, 1)
            low_e(range(EXPERTS // 2))
            gates_b(0, 0)
            rope(0, 2)
            low_e(range(EXPERTS // 2, EXPERTS))
            rope(0, 3)
            for n, each_part in enumerate(QKV_PARTS):
                low_w(EXPERTS + n, *each_part)
            dve.wait_ge(x_in[2], 16 * (NB * CHUNKS - 2))

            def body(j, last):
                for b in range(NB):
                    s = 2 * j + b
                    more = not (last and b == 1)
                    combine(s, j, b, 0, HALVES[0])
                    dve.wait_ge(cT_ps, ONE + s + 1)
                    nc.vector.tensor_copy(c9T[:, :], psQ[0:EXPERTS + 1, :]).then_inc(cT_ok, 1)
                    combine(s, j, b, 0, HALVES[1])
                    if not last:
                        norm_a(s + 2, j + 1, b)
                    if more:
                        low_x(s + 1, 1 - b)
                    combine(s, j, b, 1, ALL)
                    if not last:
                        norm_c(s + 2, j + 1, b)
                    if not more:
                        combine(s, j, b, 2, ALL)
                        combine(s, j, b, 3, ALL)
                        continue
                    if b == 1:
                        dve.wait_ge(trig_in, ONE + 32 * j + 64)
                    gates_a(s + 1, 1 - b)
                    rope(s + 1, 0)
                    combine(s, j, b, 2, HALVES[0])
                    rope(s + 1, 1)
                    combine(s, j, b, 2, HALVES[1])
                    rope(s + 1, 2)
                    combine(s, j, b, 3, HALVES[0])
                    gates_b(s + 1, 1 - b)
                    rope(s + 1, 3)
                    combine(s, j, b, 3, HALVES[1])

            with dve.Fori(0, CHUNKS - 1) as j:
                body(j, False)
            body(CHUNKS - 1, True)

        @block.tensor
        def _(pe):
            def transposes(s, b):
                pe.wait_ge(xn_ok, ONE + s + 1)
                for k in range(KC):
                    for t in range(CT):
                        ins = pe.transpose(psT[:, k, t * P:(t + 1) * P], xn[b][:, t, k * P:(k + 1) * P], ident[:, :])
                    ins.then_inc(xT_ps, 1)

            def product(out, lhs, rhs):
                todo = [(x, w, k) for x, w in ((0, 0), (0, 1), (1, 0)) for k in range(KC)]
                for n, (x, w, k) in enumerate(todo):
                    ins = pe.matmul(out, lhs(x, w, k), rhs(x, w, k), start=(n == 0), stop=(n == len(todo) - 1))
                return ins

            def product32(out, lhs, rhs):
                for k in range(KC):
                    ins = pe.matmul(out, lhs(k), rhs(k), start=(k == 0), stop=(k == KC - 1))
                return ins

            def values(s, b, first=False):
                pe.wait_ge(xT_ok, ONE + KC * (s + 1))
                pe.wait_ge(xh_ok, ONE + KC * (s + 1))
                if not first:
                    pe.wait_ge(xl_ok, ONE + KC * (s + 1))
                    pe.wait_ge(wl_ok, ONE + EXPERTS + len(QKV_PARTS))
                for t in range(CT):
                    if t >= 2:
                        pe.wait_ge(vg_ok, ONE + CT * s + t - 1)
                    out, rows = psT[:, t % 2, 0:D + GATES], slice(t * P, (t + 1) * P)
                    if first:
                        ins = product32(out, lambda k: xnT[b][:, k, rows], lambda k: wvg_sb[:, k, :])
                    else:
                        ins = product(out, lambda x, w, k: xp[b][:, x, k, rows], lambda x, w, k: wvp[:, w, k, :])
                    ins.then_inc(vg_ps, 1)

            def queries(s, b, q, first=False):
                if q > 0:
                    pe.wait_ge(qk_ok, ONE + QKT * s + q)
                cols = slice(q * P, (q + 1) * P)
                if first:
                    ins = product32(psQ[:, :], lambda k: wqk_sb[:, k, cols], lambda k: xnT[b][:, k, :])
                else:
                    ins = product(psQ[:, :], lambda x, w, k: wqp[:, w, k, cols], lambda x, w, k: xp[b][:, x, k, :])
                ins.then_inc(qk_ps, 1)

            def experts(s, b, t, banks):
                for n in banks:
                    pe.wait_ge(moe_read[n], ONE + CT * s + t)
                    if t == 0:
                        pe.wait_ge(wl_ok, ONE + 2 * (n + 1))
                    ins = product(psM[:, n, :], lambda x, w, k: xp[b][:, x, k, t * P:(t + 1) * P],
                                  lambda x, w, k: wp[:, w, k, n * 2 * D:(n + 1) * 2 * D])
                    ins.then_inc(moe_ps, 1)
                if EXPERTS // 2 - 1 in banks:
                    pe.wait_ge(bias_read, ONE + CT * s + t)
                    pe.wait_ge(cT_ok, ONE + s + 1)
                    pe.matmul(psB[:, :], c9T[:, t * P:(t + 1) * P], be_sb[:, :], start=True, stop=True
                              ).then_inc(bias_ps, 1)

            ALL = range(EXPERTS // 2)
            HALVES = (ALL[:2], ALL[2:])
            pe.wait_ge(const, ONE + 2)
            transposes(0, 0)
            pe.wait_ge(w_in, ONE + 48)
            values(0, 0, True)
            queries(0, 0, 0, True)
            pe.wait_ge(wm_ok, ONE + 1)
            for i in range(4):
                ins = pe.matmul(psM[:, i, 0:P], wrow[:, i, :], ident[:, :], start=True, stop=True)
            ins.then_inc(wm_ps, 1)
            queries(0, 0, 1, True)
            queries(0, 0, 2, True)
            queries(0, 0, 3, True)
            pe.wait_ge(w2_in[0], 16 * (EXPERTS // 2))
            pe.wait_ge(w2_in[1], 16 * (EXPERTS // 2 + 2))

            def body(j, last):
                for b in range(NB):
                    s = 2 * j + b
                    more = not (last and b == 1)
                    pe.wait_ge(xl_ok, ONE + KC * (s + 1))
                    experts(s, b, 0, ALL[:3])
                    pe.wait_ge(gate_c, ONE + s + 1)
                    pe.wait_ge(qk_ok, ONE + QKT * (s + 1))
                    for u in range(CT):
                        ins = pe.transpose(psQ[0:EXPERTS + 1, u * P:(u + 1) * P], c9[b][:, u, :], ident[:, :])
                    ins.then_inc(cT_ps, 1)
                    experts(s, b, 0, ALL[3:])
                    if more:
                        pe.wait_ge(vg_ok, ONE + CT * (s + 1))
                        transposes(s + 1, 1 - b)
                    experts(s, b, 1, ALL)
                    if not more:
                        experts(s, b, 2, ALL)
                        experts(s, b, 3, ALL)
                        continue
                    values(s + 1, 1 - b)
                    queries(s + 1, 1 - b, 0)
                    experts(s, b, 2, HALVES[0])
                    queries(s + 1, 1 - b, 1)
                    experts(s, b, 2, HALVES[1])
                    queries(s + 1, 1 - b, 2)
                    experts(s, b, 3, HALVES[0])
                    queries(s + 1, 1 - b, 3)
                    experts(s, b, 3, HALVES[1])

            with pe.Fori(0, CHUNKS - 1) as j:
                body(j, False)
            body(CHUNKS - 1, True)


def attend(nc, qk_s, v_s, wout, identf, wo, on):
    with ExitStack() as ctx:
        sb = lambda n, s, d=F32: ctx.enter_context(nc.sbuf_tensor(n, s, d))
        sems = []

        def sem(n):
            sems.append(ctx.enter_context(nc.semaphore(n)))
            return sems[-1]

        pair = lambda n: [sem(f"{n}{i}") for i in range(2)]
        each = lambda n, m: [[sem(f"{n}{i}{c}") for c in range(m)] for i in range(2)]

        Qs = [sb(f"Qs{i}", [PR + MR, CHUNKS, HG, CH], BF16) for i in range(2)]
        Ks = [sb(f"Ks{i}", [PR + MR, CHUNKS, HG, CH], BF16) for i in range(2)]
        Vs = [sb(f"Vs{i}", [P, TT, HG * VW]) for i in range(2)]
        probs = [sb(f"probs{i}", [P, HG, CH]) for i in range(2)]
        causal = sb("causal", [P, P], BF16)
        ones = sb("ones", [P, CH], BF16)
        MQ = HG * CT
        blk = sb("blk", [P, CHUNKS * MQ, 2])
        nm = sb("nm", [P, MQ])
        nmp = sb("nmp", [P, P // MQ, MQ], BF16)
        nmT = [sb(f"nmT{i}", [MR * MQ, P], BF16) for i in range(2)]
        identb = sb("identb", [P, P], BF16)
        ot = sb("ot", [P, CH])
        rs = sb("rs", [P, 2, CT, HG])

        SB = 3
        psS = ctx.enter_context(nc.psum_tensor("psS", [P, SB, CH], F32))
        psP = ctx.enter_context(nc.psum_tensor("psP", [P, 2, 2 * CH], F32))
        psO = ctx.enter_context(nc.psum_tensor("psO", [P, CH], F32))

        q_in = each("q_in", 2)
        k_in = each("k_in", 2)
        v_in = pair("v_in")
        m_in = each("m_in", CHUNKS)
        const = sem("const_b")
        blank = ctx.enter_context(nc.semaphore("blank"))
        one_rows = sem("one_rows")
        s_ps = sem("s_ps")
        s_read = [sem(f"s_read{i}") for i in range(SB)]
        masked = sem("masked")
        pv_ok = pair("pv_ok")
        o_copied = sem("o_copied")
        r_ok = sem("r_ok")
        item_ps = pair("item_ps")
        item_ok = pair("item_ok")
        m_step = sem("m_step")
        carrier = sem("carrier_b")
        pool_b = sem("pool_b")
        wo_in = sem("wo_in")

        WALK = (3, 2, 0, 1)
        FREED = {2: 1, 1: 0}

        def tiles(c):
            whole = [(i / (CT * c - 1), i) for i in range(CT * c)]
            return [kt for _, kt in sorted(whole + [((d + 0.1) / CT, CT * c + d) for d in range(CT)])]

        units = [(c, kt) for c in WALK for kt in tiles(c)]
        NU = len(units)
        diag = [kt - CT * c if kt >= CT * c else None for c, kt in units]
        q0s = [0 if d is None else d * P for d in diag]
        ends = [u for u in range(NU) if u == NU - 1 or units[u + 1][0] != units[u][0]]
        PER_BANK = [len(range(i, NU * HG, SB)) for i in range(SB)]
        PER_SLOT = NU // 2
        DG = sum(d is not None for d in diag)
        LOADS = len(BLOCKS)

        W = 2 * CH

        def of_chunk(ahead, c):
            head, full = [], []
            for qt in range(c * CT, c * CT + CT):
                k0 = W if qt * P >= W else 0
                keys = (qt + 1) * P - k0
                nh = 4 if keys <= W // 4 else 2 if keys <= W // 2 else 1
                head += [("q", ahead, qt, h, nh, k0, keys, True) for h in range(0, HG, nh)]
                if k0:
                    full += [("q", ahead, qt, h, 1, 0, W, False) for h in range(HG)]
            return head + full

        LATER = 2

        def with_m(chunks, carried):
            seq = []
            for ahead, c in chunks:
                its = of_chunk(ahead, c)
                if carried is not None:
                    its.insert(LATER, ("m",) + carried)
                seq += its
                carried = (ahead, c)
            return seq

        first_items = with_m([(1, 3), (1, 0)], None)
        NF = len(first_items)

        def schedule(more):
            queue = with_m([(0, 2), (0, 1)] + ([(1, 3), (1, 0)] if more else []), (0, 0))
            if not more:
                queue.append(("m", 0, 1))
            LAT = 200
            inf = float("inf")
            order = []
            t, act, dve, pool = 0.0, 0.0, 0.0, 0.0
            slot_free = [300.0, 1200.0]
            parts_at = {(0, 0): 0.0}
            m_at = {3: 0.0, 0: 0.0}
            s_end, read_end, pv_end, mask_end, copied = {(0, h): 0.0 for h in range(SB)}, {}, {}, {}, {}
            acts = []
            for u in range(NU):
                acts += [("e", u, h) for h in range(HG)]
                if u - 1 in ends:
                    acts.append(("c", u - 1))
            acts.append(("c", NU - 1))
            ns, nv, n_item = SB, 0, 0
            scores = NU * HG + (SB if more else 0)
            outs = []
            AHEAD = 0.04 if more else 0.3
            KEPT = 1 if more else 0
            item_total = sum(x[4] * x[6] + 70 for x in queue if x[0] == "q")
            unit_total = sum(CH - q + 60 for q in q0s)
            item_cost = unit_cost = 0
            last_q = {}
            for it in queue:
                if it[0] == "q":
                    last_q[it[1], it[2] // CT] = it
            while ns < scores or nv < NU or queue or outs or acts:
                while acts:
                    kind, u = acts[0][:2]
                    if kind == "e":
                        h = acts[0][2]
                        if (u, h) not in s_end or (u >= 2 and u - 2 not in pv_end):
                            break
                        act = max(act, s_end[u, h] + LAT, pv_end.get(u - 2, 0.0) + LAT) + (CH - q0s[u]) * 0.833 + 60
                        read_end[u, h] = act
                        if h == HG - 1:
                            if diag[u] is not None:
                                pool = max(pool, act + LAT) + 700
                                mask_end[u] = pool
                            else:
                                mask_end[u] = act
                    else:
                        if u not in pv_end:
                            break
                        act = max(act, pv_end[u] + LAT) + 490
                        copied[u] = act
                        outs.append(u)
                    acts.pop(0)
                n = n_item
                slot = n % 2
                item, item_at = None, inf
                if outs and (copied[outs[0]] + LAT <= max(t, slot_free[slot]) or not queue):
                    item, item_at = ("o", 0, units[outs[0]][0]), max(slot_free[slot], copied[outs[0]] + LAT)
                elif queue and (len(queue) > KEPT or nv == NU):
                    item = queue[0]
                    item_at = slot_free[slot]
                    if item[0] == "m":
                        item_at = max(item_at, parts_at[item[1:]] + LAT)
                s_at = pv_at = inf
                if ns < scores:
                    u, h = divmod(ns, HG)
                    s_at = 0.0
                    if u == NU:
                        before = max(n for n in range(NU * HG) if n % SB == h)
                        s_at = max(read_end.get(divmod(before, HG), inf) + LAT, m_at.get(-1, inf))
                    else:
                        s_at = read_end.get(divmod(ns - SB, HG), inf) + LAT
                        if units[u][1] == 0:
                            s_at = max(s_at, m_at.get(units[u][0], inf))
                if nv < NU:
                    pv_at = mask_end.get(nv, inf) + LAT
                    if units[nv][1] == 0 and nv:
                        pv_at = max(pv_at, copied.get(nv - 1, inf) + LAT)
                t = max(t, min(item_at, s_at, pv_at))
                early = item_cost > (AHEAD + unit_cost / unit_total) * item_total
                starved = s_at <= t and act < t + 300
                if item_at <= t and not ((early or starved) and min(s_at, pv_at) <= t):
                    if item[0] == "q":
                        cols = item[4] * item[6]
                        cost, work = cols * 0.417 + (60 * item[4] if item[7] else 0) + 20, cols * 1.042 + 70
                    elif item[0] == "m":
                        cost, work = 60, 200
                    else:
                        cost, work = 480, 900
                    t += cost
                    dve = max(dve, t + LAT) + work
                    slot_free[slot] = dve + LAT
                    if item[0] == "m":
                        m_at[item[2] if item[1] == 0 else -1] = dve + 2500
                    if item[0] == "q":
                        item_cost += item[4] * item[6] + 70
                        if last_q[item[1], item[2] // CT] is item:
                            dve += 1000
                            parts_at[item[1], item[2] // CT] = dve
                    outs.pop(0) if item[0] == "o" else queue.pop(0)
                    order.append(item)
                    n_item += 1
                elif pv_at <= t and not s_at <= t:
                    t += (CH - q0s[nv]) * 1.75 + 30
                    unit_cost += CH - q0s[nv] + 60
                    pv_end[nv] = t
                    order.append(("pv", nv))
                    nv += 1
                else:
                    t += (CH - q0s[ns // HG % NU]) * 0.417 + 5
                    s_end[divmod(ns, HG)] = t
                    order.append(("s",) + divmod(ns, HG))
                    ns += 1
            return order

        orders = {more: schedule(more) for more in (True, False)}
        is_item = lambda x: x[0] in "qmo"
        lists = {more: [x for x in orders[more] if is_item(x)] for more in orders}
        NI = len(lists[True])
        assert NI % 2 == 0
        M_PARTS = {(0, 2): 2, (0, 1): 3, (1, 3): 4, (1, 0): 5}
        M_TURN = {(0, 0): 1, (0, 2): 2, (0, 1): 3, (1, 3): 4}

        def slot_of(n):
            return (NF + n) % 2

        def uses(g, n):
            return NI // 2 * g + (NF + n) // 2

        block = ctx.enter_context(nc.Block())

        @block.sync
        def _(sp):
            def rows_of(n):
                first = sum(m for m, _ in BLOCKS[:n]) * HD
                return slice(first, first + BLOCKS[n][0] * HD)

            HC = CHUNKS // 2

            def load_q(g, r, half):
                cs = slice(half * HC, (half + 1) * HC)
                for i, (n, p) in enumerate(BLOCKS):
                    sp.dma_start(Qs[r][rows_of(i), cs, :, :].rearrange("r c h n -> r (c h n)"),
                                 qk_s[0, g, 0:n, :, cs, :, :].rearrange("p d c h n -> (p d) (c h n)")
                                 ).then_inc(q_in[r][half], 16)

            def load_k(g, r, half):
                cs = slice(half * HC, (half + 1) * HC)
                for i, (n, p) in enumerate(BLOCKS):
                    src = qk_s[1, g, p, :, cs, :, :].rearrange("d c h n -> d (c h n)")
                    sp.dma_start(Ks[r][rows_of(i), cs, :, :].rearrange("r c h n -> r (c h n)"),
                                 src.unsqueeze(0).to_broadcast([n, HD, HC * HG * CH])).then_inc(k_in[r][half], 16)

            def load_v(g, r, half):
                ts = slice(half * HC * CT, (half + 1) * HC * CT)
                sp.dma_start(Vs[r][:, ts, :], v_s[g, :, ts, :]).then_inc(v_in[r], 16)

            def load(g, r, half):
                load_q(g, r, half)
                load_k(g, r, half)
                load_v(g, r, half)

            def store_m(slot, count, turn, r, c):
                sp.wait_ge(item_ok[slot], ONE + count + 1)
                sp.dma_start(Qs[r][PR:PR + MR, c, :, :].rearrange("r h n -> r (h n)"),
                             nmT[turn % 2][:, :]).then_inc(m_in[r][c], 16)

            load_k(0, 0, 1)
            load_q(0, 0, 1)
            load_k(0, 0, 0)
            load_q(0, 0, 0)
            load_v(0, 0, 0)
            load_v(0, 0, 1)
            n = first_items.index(("m", 1, 3))
            store_m(n % 2, n // 2, 0, 0, 3)
            load(1, 1, 1)
            load(1, 1, 0)
            sp.dma_start(wo[:, :, :], wout.rearrange("(k p) n -> p k n", p=P)).then_inc(wo_in, 16)

            def body(j, last):
                for r in range(2):
                    g = 2 * j + r
                    more = not (last and r == 1)
                    n = 0
                    for x in orders[more]:
                        if x[0] == "m":
                            store_m(slot_of(n), uses(g, n), M_TURN[x[1:]], r ^ x[1], x[2])
                        elif x[0] == "pv" and x[1] in ends and units[x[1]][0] in FREED and not last:
                            u = x[1]
                            sp.wait_ge(pv_ok[u % 2], ONE + PER_SLOT * g + u // 2 + 1)
                            sp.sem_inc(carrier, 1)
                            load(g + 2, r, FREED[units[u][0]])
                        n += is_item(x)

            with sp.Fori(0, GROUPS // 2 - 1) as j:
                body(j, False)
            body(GROUPS // 2 - 1, True)
            sp.wait_ge(wo_in, ONE + 16)

        @block.gpsimd
        def _(pool):
            for every in sems:
                pool.sem_inc(every, ONE)
            nc.gpsimd.memset(causal[:, :], 0.0).then_inc(pool_b, 1)
            nc.gpsimd.memset(identb[:, :], 0.0).then_inc(pool_b, 1)
            nc.gpsimd.memset(identf[:, :], 0.0).then_inc(pool_b, 1)
            pool.wait_ge(pool_b, ONE + 3)
            nc.gpsimd.affine_select(out=causal[:, :], in_=causal[:, :], compare_op=ALU.is_ge, fill=LOW, base=0,
                                    pattern=[[-1, P]], channel_multiplier=1).then_inc(const, 1)
            for eye in (identb, identf):
                nc.gpsimd.affine_select(out=eye[:, :], in_=eye[:, :], compare_op=ALU.not_equal, fill=1.0, base=0,
                                        pattern=[[-1, P]], channel_multiplier=1).then_inc(const, 1)

            def body(j):
                for r in range(2):
                    g = 2 * j + r
                    for u, (c, kt) in enumerate(units):
                        if diag[u] is not None:
                            for h in range(HG):
                                n = u * HG + h
                                pool.wait_ge(s_read[n % SB], ONE + PER_BANK[n % SB] * g + n // SB + 1)
                            v = probs[u % 2][:, :, q0s[u]:q0s[u] + P]
                            pool.sem_inc(carrier, 1)
                            nc.gpsimd.affine_select(out=v, in_=v, compare_op=ALU.is_ge, fill=0.0, base=0,
                                                    pattern=[[0, HG], [1, P]], channel_multiplier=-1
                                                    ).then_inc(masked, 1)

            with pool.Fori(0, GROUPS // 2) as j:
                body(j)

        @block.scalar
        def _(act):
            act.wait_ge(blank, 1)
            for r in range(2):
                nc.scalar.copy(Ks[r][PR:PR + MR, :, :, :].rearrange("r c h n -> r (c h) n"),
                               ones[PR:PR + MR, :].unsqueeze(1).to_broadcast([MR, CHUNKS * HG, CH])
                               ).then_inc(one_rows, 1)

            def body(j):
                for r in range(2):
                    g = 2 * j + r

                    def copy_out(n):
                        u = ends[n]
                        act.wait_ge(pv_ok[u % 2], ONE + PER_SLOT * g + u // 2 + 1)
                        act.wait_ge(r_ok, ONE + CHUNKS * g + n)
                        nc.scalar.copy(ot[:, :], psO[:, :]).then_inc(o_copied, 1)

                    for u, (c, kt) in enumerate(units):
                        q0 = q0s[u]
                        act.wait_ge(pv_ok[u % 2], ONE + PER_SLOT * g + u // 2)
                        for h in range(HG):
                            n = u * HG + h
                            act.wait_ge(s_ps, ONE + NU * HG * g + n + 1)
                            nc.scalar.activation(probs[u % 2][:, h, q0:CH], psS[:, n % SB, q0:CH], ACT.Exp,
                                                 scale=SCALE).then_inc(s_read[n % SB], 1)
                        if u - 1 in ends:
                            copy_out(ends.index(u - 1))
                    copy_out(CHUNKS - 1)

            with act.Fori(0, GROUPS // 2) as j:
                body(j)

        @block.vector
        def _(dve):
            MS = 5

            def parts(turn, c, waits):
                at = MS * turn
                for slot, count in waits:
                    dve.wait_ge(item_ok[slot], ONE + count + 1)
                nc.vector.tensor_reduce(nm[:, :], blk[:, c * MQ:(c + 1) * MQ, :], AX.X, ALU.max, negate=True
                                        ).then_inc(m_step, 1)
                dve.wait_ge(m_step, ONE + at + 1)
                nc.vector.tensor_copy(nmp[:, 0, :], nm[:, :]).then_inc(m_step, 1)
                dve.wait_ge(m_step, ONE + at + 2)
                nc.vector.tensor_tensor(nm[:, :], nm[:, :], nmp[:, 0, :], ALU.subtract).then_inc(m_step, 1)
                dve.wait_ge(m_step, ONE + at + 3)
                nc.vector.tensor_copy(nmp[:, 1, :], nm[:, :]).then_inc(m_step, 1)
                dve.wait_ge(m_step, ONE + at + 4)
                nc.vector.tensor_tensor(nmp[:, 2, :], nm[:, :], nmp[:, 1, :], ALU.subtract).then_inc(m_step, 1)

            def reduce(item, slot):
                _, _, qt, h, nh, k0, keys, last = item
                row = qt // CT * MQ + h * CT + qt % CT
                nc.vector.tensor_reduce(blk[:, row:row + (nh - 1) * CT + 1:CT, int(last)],
                                        psP[:, slot, :].rearrange("p (h n) -> p h n", h=nh)[:, :, 0:keys],
                                        AX.X, ALU.max).then_inc(item_ok[slot], 1)

            def turned(slot, turn):
                nc.vector.tensor_copy(nmT[turn % 2][:, :], psP[0:MR * MQ, slot, :].bitcast(BF16)[:, 0:P]
                                      ).then_inc(item_ok[slot], 1)

            def normalise(j, r, n, c, slot):
                at = CHUNKS * (2 * j + r) + n
                t = psP[:, slot, 0:CH].rearrange("p (t h w) -> p t h w", t=CT, h=HG)
                nc.vector.reciprocal(rs[:, n % 2, :, :], t[:, :, :, HD]).then_inc(r_ok, 1)
                dve.wait_ge(r_ok, ONE + at + 1)
                dst = on[:, bass.ds(j, 1), c * CT:(c + 1) * CT, r * GR:(r + 1) * GR].rearrange("p o t (h w) -> p (o t) h w", h=HG)
                nc.vector.tensor_tensor(dst, t[:, :, :, 0:HD],
                                        rs[:, n % 2, :, :].unsqueeze(3).to_broadcast([P, CT, HG, HD]), ALU.mult
                                        ).then_inc(item_ok[slot], 1)

            nc.vector.memset(ones[:, :], 1.0).then_inc(blank, 1)
            nc.vector.memset(blk[:, :, :], LOW).then_inc(blank, 1)
            nc.vector.memset(nmp[:, :, :], 0.0).then_inc(blank, 1)
            dve.wait_ge(blank, 3)
            for n, item in enumerate(first_items):
                dve.wait_ge(item_ps[n % 2], ONE + n // 2 + 1)
                if item[0] == "m":
                    turned(n % 2, 0)
                    continue
                reduce(item, n % 2)
                c = item[2] // CT
                if not any(x[0] == "q" and x[2] // CT == c for x in first_items[n + 1:]):
                    parts((3, 0).index(c), c, [(k % 2, k // 2) for k in (n - 1, n)])

            def body(j, last):
                for r in range(2):
                    g = 2 * j + r
                    more = not (last and r == 1)
                    items = lists[more]
                    for n, item in enumerate(items):
                        slot = slot_of(n)
                        dve.wait_ge(item_ps[slot], ONE + uses(g, n) + 1)
                        if item[0] == "q":
                            reduce(item, slot)
                            key = (item[1], item[2] // CT)
                            if not any(x[0] == "q" and (x[1], x[2] // CT) == key for x in items[n + 1:]):
                                parts(4 * g + M_PARTS[key], key[1], [(slot_of(k), uses(g, k)) for k in (n - 1, n)])
                        elif item[0] == "m":
                            ahead, c = item[1:]
                            if c == 0:
                                dve.wait_ge(m_in[1 - r][1], ONE + 16 * (j + r))
                            elif c == 2:
                                dve.wait_ge(m_in[r][3], ONE + 16 * (j + 1))
                            elif c == 1:
                                dve.wait_ge(m_in[r][0], ONE + 16 * (j + 1))
                            else:
                                dve.wait_ge(m_in[r][2], ONE + 16 * (j + 1))
                            turned(slot, M_TURN[item[1:]])
                        else:
                            normalise(j, r, WALK.index(item[2]), item[2], slot)

            with dve.Fori(0, GROUPS // 2 - 1) as j:
                body(j, False)
            body(GROUPS // 2 - 1, True)

        @block.tensor
        def _(pe):
            def scores_q(item, slot, r):
                _, _, qt, h0, nh, k0, keys, last = item
                for i in range(nh):
                    h, at = h0 + i, i * (W // nh)
                    q = Qs[r][0:PR, qt // CT, h, qt % CT * P:(qt % CT + 1) * P]
                    cuts = [k for k in (0, CH) if k < keys - (P if last else 0)]
                    for k in cuts:
                        w = min(CH, keys - (P if last else 0) - k)
                        c, off = divmod(k0 + k, CH)
                        ins = pe.matmul(psP[:, slot, at + k:at + k + w], q, Ks[r][0:PR, c, h, off:off + w],
                                        start=True, stop=True)
                    if last:
                        k = keys - P
                        c, off = divmod(k0 + k, CH)
                        pe.matmul(psP[:, slot, at + k:at + k + P], q, Ks[r][0:PR, c, h, off:off + P],
                                  start=True, stop=False)
                        ins = pe.matmul(psP[:, slot, at + k:at + k + P], identb[:, :], causal[:, :],
                                        start=False, stop=True)
                ins.then_inc(item_ps[slot], 1)

            def turn_m(slot, turn):
                pe.wait_ge(m_step, ONE + 5 * (turn + 1))
                pe.sem_inc(carrier, 1)
                pe.transpose(psP[:, slot, :].bitcast(BF16)[:, 0:P], nmp[:, :, :].rearrange("p m n -> p (m n)"),
                             identb[:, :]).then_inc(item_ps[slot], 1)

            def arrived(count, r, of_q, of_k):
                for half in of_q:
                    pe.wait_ge(q_in[r][half], ONE + 16 * LOADS * count)
                for half in of_k:
                    pe.wait_ge(k_in[r][half], ONE + 16 * LOADS * count)

            pe.wait_ge(const, ONE + 3)
            arrived(1, 0, (1,), (1,))
            for n, item in enumerate(first_items):
                pe.wait_ge(item_ok[n % 2], ONE + n // 2)
                if item[0] == "m":
                    turn_m(n % 2, 0)
                    continue
                if n == [x[0] == "q" and x[5] == 0 for x in first_items].index(True):
                    arrived(1, 0, (0,), (0,))
                scores_q(item, n % 2, 0)

            def scores(g, j, r, u, h):
                n, q0 = u * HG + h, q0s[u]
                c, kt = units[u]
                if h == 0 and kt == 0:
                    pe.wait_ge(m_in[r][c], ONE + 16 * (j + 1))
                pe.wait_ge(s_read[n % SB], ONE + PER_BANK[n % SB] * g + n // SB)
                pe.matmul(psS[:, n % SB, q0:CH], Ks[r][:, kt // CT, h, kt % CT * P:(kt % CT + 1) * P],
                          Qs[r][:, c, h, q0:CH], start=True, stop=True).then_inc(s_ps, 1)

            pe.wait_ge(one_rows, ONE + 2)
            for h in range(SB):
                scores(0, 0, 0, 0, h)

            def body(j, last):
                for r in range(2):
                    g = 2 * j + r
                    more = not (last and r == 1)

                    def pv(u):
                        c, kt = units[u]
                        q0, end = q0s[u], u in ends
                        if diag[u] is None:
                            for h in range(HG):
                                n = u * HG + h
                                pe.wait_ge(s_read[n % SB], ONE + PER_BANK[n % SB] * g + n // SB + 1)
                        else:
                            pe.wait_ge(masked, ONE + DG * g + sum(d is not None for d in diag[:u]) + 1)
                        if kt == 0:
                            pe.wait_ge(o_copied, ONE + CHUNKS * g + WALK.index(c))
                        for h in range(HG):
                            ins = pe.matmul(psO[h * VW:(h + 1) * VW, q0:CH], Vs[r][:, kt, h * VW:(h + 1) * VW],
                                            probs[u % 2][:, h, q0:CH], start=(kt == 0), stop=end,
                                            tile_position=(0, h * VW))
                        ins.then_inc(pv_ok[u % 2], 1)

                    pe.wait_ge(v_in[r], ONE + 16 * 2 * (j + 1))
                    n, here = 0, False
                    for x in orders[more]:
                        if x[0] == "s":
                            if x[1] < NU:
                                scores(g, j, r, x[1], x[2])
                            else:
                                scores(g + 1, j + r, 1 - r, 0, x[2])
                            continue
                        if x[0] == "pv":
                            pv(x[1])
                            continue
                        slot = slot_of(n)
                        if x[0] == "q" and x[1] == 1 and not here:
                            arrived(j + r + 1, 1 - r, (0, 1), (0, 1))
                            here = True
                        pe.wait_ge(item_ok[slot], ONE + uses(g, n))
                        if x[0] == "q":
                            scores_q(x, slot, r ^ x[1])
                        elif x[0] == "m":
                            turn_m(slot, 4 * g + M_TURN[x[1:]])
                        else:
                            pe.wait_ge(o_copied, ONE + CHUNKS * g + WALK.index(x[2]) + 1)
                            for t in range(CT):
                                ins = pe.transpose(psP[:, slot, t * P:(t + 1) * P], ot[:, t * P:(t + 1) * P],
                                                   identf[:, :])
                            ins.then_inc(item_ps[slot], 1)
                        n += 1

            with pe.Fori(0, GROUPS // 2 - 1) as j:
                body(j, False)
            body(GROUPS // 2 - 1, True)


def output(nc, wo, ident, acc, on, out):
    with ExitStack() as ctx:
        sem = lambda n: ctx.enter_context(nc.semaphore(n))
        aT = [ctx.enter_context(nc.sbuf_tensor(f"aT{i}", [P, KC, P], F32)) for i in range(2)]
        psT = ctx.enter_context(nc.psum_tensor("psT_c", [P, 4, CH], F32))
        ps = ctx.enter_context(nc.psum_tensor("ps", [P, 4, CH], F32))
        t_ps = sem("t_ps")
        t_ok = sem("t_ok")
        o_ps = sem("o_ps")
        o_add = sem("o_add")
        o_out = sem("o_out")
        block = ctx.enter_context(nc.Block())

        @block.sync
        def _(sp):
            for c in range(TILES // CT):
                sp.wait_ge(o_add, CT * (c + 1))
                sp.dma_start(out[c // CHUNKS, c % CHUNKS * CH:(c % CHUNKS + 1) * CH, :]
                             .rearrange("(t p) d -> p t d", p=P), acc[:, c * CT:(c + 1) * CT, :]).then_inc(o_out, 16)
            sp.wait_ge(o_out, 16 * TILES // CT)

        @block.tensor
        def _(pe):
            def turn(t):
                if t >= 4:
                    pe.wait_ge(t_ok, t - 3)
                for k in range(KC):
                    ins = pe.transpose(psT[:, t % 4, k * P:(k + 1) * P], on[:, t // TT * KC + k, t % TT, :], ident[:, :])
                ins.then_inc(t_ps, 1)

            turn(0)
            for t in range(TILES):
                if t + 1 < TILES:
                    turn(t + 1)
                pe.wait_ge(t_ok, t + 1)
                if t >= 4:
                    pe.wait_ge(o_add, t - 3)
                for k in range(KC):
                    ins = pe.matmul(ps[:, t % 4, 0:D], aT[t % 2][:, k, :], wo[:, k, :],
                                    start=(k == 0), stop=(k == KC - 1))
                ins.then_inc(o_ps, 1)

        @block.scalar
        def _(act):
            for t in range(TILES):
                act.wait_ge(t_ps, t + 1)
                if t >= 2:
                    act.wait_ge(o_ps, t - 1)
                nc.scalar.copy(aT[t % 2][:, :, :].rearrange("p k n -> p (k n)"), psT[:, t % 4, 0:D]).then_inc(t_ok, 1)

        @block.vector
        def _(dve):
            for t in range(TILES):
                dve.wait_ge(o_ps, t + 1)
                nc.vector.tensor_tensor(acc[:, t, :], ps[:, t % 4, 0:D], acc[:, t, :], ALU.add).then_inc(o_add, 1)


def build(nc, x, wqk, wvg, wout, bout, gb, we, be, cos, sin, out):
    qk_s = nc.dram_tensor("qk_scratch", [2, GROUPS, 3, HD, CHUNKS, HG, CH], BF16, kind="Internal").ap()
    v_s = nc.dram_tensor("v_scratch", [GROUPS, P, TT, HG * VW], F32, kind="Internal").ap()
    with nc.sbuf_tensor("acc", [P, TILES, D], F32) as acc:
        project(nc, x, wqk, wvg, we, be, bout, gb, cos, sin, qk_s, v_s, acc)
        with nc.sbuf_tensor("on", [P, B * KC, TT, P], F32) as on, nc.sbuf_tensor("wo", [P, KC, D], F32) as wo, \
                nc.sbuf_tensor("identf", [P, P], F32) as identf:
            attend(nc, qk_s, v_s, wout, identf, wo, on)
            output(nc, wo, identf, acc, on, out)


def rotary_tables():
    inv = (1.0 / np.float32(10000.0) ** (np.arange(0, HD, 2, dtype=np.float32) / np.float32(HD))).astype(np.float32)
    f = np.arange(N, dtype=np.float32)[None, :] * np.tile(np.repeat(inv, 2), P // HD)[:, None]
    sign = np.where(np.arange(P) % 2 == 0, -1.0, 1.0).astype(np.float32)[:, None]
    return np.cos(f).astype(np.float32), (np.sin(f) * sign).astype(np.float32)


def kernel(L0_attn_X, L0_attn_Wqkv, L0_attn_Wout, L0_attn_bout, L0_ffn_gate_w, L0_ffn_gate_b, L0_ffn_expert_w,
           L0_ffn_expert_b):
    import concourse.bacc as bacc
    from concourse.bass_utils import run_bass_kernel_spmd

    wqkv = np.asarray(L0_attn_Wqkv)
    cos, sin = rotary_tables()
    arrays = {
        "x": np.ascontiguousarray(L0_attn_X),
        "wqk": np.ascontiguousarray(wqkv[:, :2 * D]),
        "wvg": np.ascontiguousarray(np.concatenate([wqkv[:, 2 * D:], np.asarray(L0_ffn_gate_w).T], axis=1)),
        "wout": np.ascontiguousarray(L0_attn_Wout),
        "bout": np.asarray(L0_attn_bout).reshape(1, D),
        "gb": np.asarray(L0_ffn_gate_b).reshape(1, GATES),
        "we": np.ascontiguousarray(L0_ffn_expert_w),
        "be": np.ascontiguousarray(L0_ffn_expert_b),
        "cos": cos,
        "sin": sin,
    }
    nc = bacc.Bacc("TRN2", target_bir_lowering=False, num_devices=1)
    args = [nc.dram_tensor(n, a.shape, mybir.dt.from_np(a.dtype), kind="ExternalInput").ap()
            for n, a in arrays.items()]
    out = nc.dram_tensor("out", (B, N, D), F32, kind="ExternalOutput").ap()
    build(nc, *args, out)
    r = run_bass_kernel_spmd(nc, [arrays], core_ids=[0])
    return r.results[0]["out"]
```
